# Optimizing a Trainium2 kernel written in Bass

```python
import numpy as np
import jax
import jax.numpy as jnp

def _softmax(x, axis=-1):
    return jax.nn.softmax(x, axis=axis)

def _gelu(x):
    return jax.nn.gelu(x, approximate=True)

def _silu(x):
    return jax.nn.silu(x)

def _sigmoid(x):
    return jax.nn.sigmoid(x)

def _layernorm(x, axis=-1, eps=1e-05):
    m = jnp.mean(x, axis=axis, keepdims=True)
    v = jnp.var(x, axis=axis, keepdims=True)
    return (x - m) / jnp.sqrt(v + eps)

def _scatter_add(tgt, idx, src, axis=0):
    return tgt.at[idx].add(src)

def _segment_sum(src, seg, n):
    return jax.ops.segment_sum(src, seg, n)
kernel_name = 'mk_xattn_seq_d2_seqx_r4_98caf2'

def setup_inputs(seed: int=0):
    np.random.seed(seed)
    _w = jnp.asarray

    def _rec_inputs():
        import jax
        import jax.numpy as jnp
        _rk = jax.random.key(seed)
        x = 0.0003765 + 1 * jax.random.normal(jax.random.fold_in(_rk, 1), (16, 256, 256), jnp.float32)
        _lenS = 256 - jax.random.randint(jax.random.fold_in(_rk, 7), (16,), 0, max(1, 256 // 4) + 1, jnp.int32)
        _lenS2 = 256 - jax.random.randint(jax.random.fold_in(_rk, 8), (16,), 0, max(1, 256 // 4) + 1, jnp.int32)
        _ctx_1024P = jax.random.normal(jax.random.fold_in(_rk, 11), (16, 16, 256), jnp.float32)
        _ctx_1024c = jax.random.dirichlet(jax.random.fold_in(_rk, 511), 0.3 * jnp.ones((16,), jnp.float32), (16, 256))
        _ctx_1024t = jnp.einsum('bsk,bkd->bsd', _ctx_1024c, _ctx_1024P)
        _ctx_1024t = _ctx_1024t * jax.lax.rsqrt(jnp.mean(jnp.square(_ctx_1024t)) + 1e-12) * 0.953939
        ctx_1024 = -0.000292821 + 1.00034 * (_ctx_1024t + 0.3 * jax.random.normal(jax.random.fold_in(_rk, 611), (16, 256, 256), jnp.float32))
        _validS = jnp.arange(256)[None, :] < _lenS[:, None]
        _validS2 = jnp.arange(256)[None, :] < _lenS2[:, None]
        _causal = jnp.tril(jnp.ones((256, 256), dtype=bool))
        mask_Bx1x1xS2_if1 = jnp.where(jnp.ones((16, 1, 1, 256), dtype=bool), 1, 0).astype(jnp.int32)
        mask_1x1xSxS_bk0 = jnp.logical_not(jnp.broadcast_to(_validS[0:1, None, None, :], (1, 1, 256, 256)))
        return (x, ctx_1024, mask_Bx1x1xS2_if1, mask_1x1xSxS_bk0)
    x, ctx_1024, mask_Bx1x1xS2_if1, mask_1x1xSxS_bk0 = _rec_inputs()

    def _L0_xattn_setup():
        import jax, jax.numpy as jnp
        import numpy as np
        EMBED = 256
        HEADS = 16
        HEAD_DIM = EMBED // HEADS
        FF = 4 * EMBED
        EPS = 1e-05

        def layernorm(x, g, b):
            mu = jnp.mean(x, axis=-1, keepdims=True)
            var = jnp.mean((x - mu) ** 2, axis=-1, keepdims=True)
            return (x - mu) * jax.lax.rsqrt(var + EPS) * g + b
        key = jax.random.key(seed)
        ks = jax.random.split(key, 16)
        B, S = (2, 512)
        f32 = jnp.float32
        inp = {'value': jax.random.normal(ks[0], (B, S, EMBED), f32), 'key': jax.random.normal(ks[1], (B, S, EMBED), f32), 'query': jax.random.normal(ks[2], (B, S, EMBED), f32), 'mask': jnp.ones((B, 1, 1, S), jnp.int32), 'wv': jax.random.normal(ks[3], (HEAD_DIM, HEAD_DIM), f32) * 0.02, 'wk': jax.random.normal(ks[4], (HEAD_DIM, HEAD_DIM), f32) * 0.02, 'wq': jax.random.normal(ks[5], (HEAD_DIM, HEAD_DIM), f32) * 0.02, 'w_out': jax.random.normal(ks[6], (EMBED, EMBED), f32) * 0.02, 'b_out': jnp.zeros((EMBED,), f32), 'g1': jnp.ones((EMBED,), f32), 'beta1': jnp.zeros((EMBED,), f32), 'w_ff1': jax.random.normal(ks[7], (EMBED, FF), f32) * 0.02, 'b_ff1': jnp.zeros((FF,), f32), 'w_ff2': jax.random.normal(ks[8], (FF, EMBED), f32) * 0.02, 'b_ff2': jnp.zeros((EMBED,), f32), 'g2': jnp.ones((EMBED,), f32), 'beta2': jnp.zeros((EMBED,), f32)}
        return inp
    _L0_xattn_all = _L0_xattn_setup()
    _L0_xattn_in = {k: v for k, v in _L0_xattn_all.items() if k in ('wv', 'wk', 'wq', 'w_out', 'b_out', 'g1', 'beta1', 'w_ff1', 'b_ff1', 'w_ff2', 'b_ff2', 'g2', 'beta2')}
    del _L0_xattn_all

    def _L1_xattn_setup():
        import jax, jax.numpy as jnp
        import numpy as np
        EMBED_DIM = 256
        NUM_HEADS = 16
        HEAD_DIM = EMBED_DIM // NUM_HEADS
        FF_DIM = 1024
        B, T, S = (2, 512, 512)
        LN_EPS = 1e-05

        def _layernorm(x, g, b):
            mu = jnp.mean(x, -1, keepdims=True)
            var = jnp.mean(jnp.square(x - mu), -1, keepdims=True)
            return (x - mu) * jax.lax.rsqrt(var + LN_EPS) * g + b

        def _mha(q_in, k_in, v_in, wq, bq, wk, bk, wv, bv, wo, bo, mask=None):
            Bq, Tq, C = q_in.shape
            Tk = k_in.shape[1]
            Q = (q_in @ wq + bq).reshape(Bq, Tq, NUM_HEADS, HEAD_DIM)
            K = (k_in @ wk + bk).reshape(Bq, Tk, NUM_HEADS, HEAD_DIM)
            V = (v_in @ wv + bv).reshape(Bq, Tk, NUM_HEADS, HEAD_DIM)
            scores = jnp.einsum('bqhd,bkhd->bhqk', Q, K) / np.sqrt(HEAD_DIM)
            if mask is not None:
                scores = jnp.where(mask, scores, -jnp.inf)
            attn = jax.nn.softmax(scores, axis=-1)
            out = jnp.einsum('bhqk,bkhd->bqhd', attn, V).reshape(Bq, Tq, C)
            return out @ wo + bo
        key = jax.random.key(seed)
        ks = jax.random.split(key, 20)
        sd = 1.0 / np.sqrt(EMBED_DIM)
        d = {'x': jax.random.normal(ks[0], (B, T, EMBED_DIM), jnp.float32), 'encoder_outputs': jax.random.normal(ks[1], (B, S, EMBED_DIM), jnp.float32), 'tgt_mask': jnp.tril(jnp.ones((T, T), bool))[None, None]}
        names = ['sa_wq', 'sa_wk', 'sa_wv', 'sa_wo', 'ca_wq', 'ca_wk', 'ca_wv', 'ca_wo']
        for i, n in enumerate(names):
            d[n] = jax.random.normal(ks[2 + i], (EMBED_DIM, EMBED_DIM), jnp.float32) * sd
            d[n.replace('w', 'b')] = jnp.zeros((EMBED_DIM,), jnp.float32)
        d['ff_w1'] = jax.random.normal(ks[10], (EMBED_DIM, FF_DIM), jnp.float32) * sd
        d['ff_b1'] = jnp.zeros((FF_DIM,), jnp.float32)
        d['ff_w2'] = jax.random.normal(ks[11], (FF_DIM, EMBED_DIM), jnp.float32) * (1.0 / np.sqrt(FF_DIM))
        d['ff_b2'] = jnp.zeros((EMBED_DIM,), jnp.float32)
        for i in (1, 2, 3):
            d[f'ln{i}_g'] = jnp.ones((EMBED_DIM,), jnp.float32)
            d[f'ln{i}_b'] = jnp.zeros((EMBED_DIM,), jnp.float32)
        return d
    _L1_xattn_all = _L1_xattn_setup()
    _L1_xattn_in = {k: v for k, v in _L1_xattn_all.items() if k in ('sa_wq', 'sa_bq', 'sa_wk', 'sa_bk', 'sa_wv', 'sa_bv', 'sa_wo', 'sa_bo', 'ca_wq', 'ca_bq', 'ca_wk', 'ca_bk', 'ca_wv', 'ca_bv', 'ca_wo', 'ca_bo', 'ff_w1', 'ff_b1', 'ff_w2', 'ff_b2', 'ln1_g', 'ln1_b', 'ln2_g', 'ln2_b', 'ln3_g', 'ln3_b')}
    del _L1_xattn_all
    return {'x': x, 'ctx_1024': ctx_1024, 'mask_Bx1x1xS2_if1': mask_Bx1x1xS2_if1, 'mask_1x1xSxS_bk0': mask_1x1xSxS_bk0, 'L0_xattn_wv': _L0_xattn_in['wv'], 'L0_xattn_wk': _L0_xattn_in['wk'], 'L0_xattn_wq': _L0_xattn_in['wq'], 'L0_xattn_w_out': _L0_xattn_in['w_out'], 'L0_xattn_b_out': _L0_xattn_in['b_out'], 'L0_xattn_g1': _L0_xattn_in['g1'], 'L0_xattn_beta1': _L0_xattn_in['beta1'], 'L0_xattn_w_ff1': _L0_xattn_in['w_ff1'], 'L0_xattn_b_ff1': _L0_xattn_in['b_ff1'], 'L0_xattn_w_ff2': _L0_xattn_in['w_ff2'], 'L0_xattn_b_ff2': _L0_xattn_in['b_ff2'], 'L0_xattn_g2': _L0_xattn_in['g2'], 'L0_xattn_beta2': _L0_xattn_in['beta2'], 'L1_xattn_sa_wq': _L1_xattn_in['sa_wq'], 'L1_xattn_sa_bq': _L1_xattn_in['sa_bq'], 'L1_xattn_sa_wk': _L1_xattn_in['sa_wk'], 'L1_xattn_sa_bk': _L1_xattn_in['sa_bk'], 'L1_xattn_sa_wv': _L1_xattn_in['sa_wv'], 'L1_xattn_sa_bv': _L1_xattn_in['sa_bv'], 'L1_xattn_sa_wo': _L1_xattn_in['sa_wo'], 'L1_xattn_sa_bo': _L1_xattn_in['sa_bo'], 'L1_xattn_ca_wq': _L1_xattn_in['ca_wq'], 'L1_xattn_ca_bq': _L1_xattn_in['ca_bq'], 'L1_xattn_ca_wk': _L1_xattn_in['ca_wk'], 'L1_xattn_ca_bk': _L1_xattn_in['ca_bk'], 'L1_xattn_ca_wv': _L1_xattn_in['ca_wv'], 'L1_xattn_ca_bv': _L1_xattn_in['ca_bv'], 'L1_xattn_ca_wo': _L1_xattn_in['ca_wo'], 'L1_xattn_ca_bo': _L1_xattn_in['ca_bo'], 'L1_xattn_ff_w1': _L1_xattn_in['ff_w1'], 'L1_xattn_ff_b1': _L1_xattn_in['ff_b1'], 'L1_xattn_ff_w2': _L1_xattn_in['ff_w2'], 'L1_xattn_ff_b2': _L1_xattn_in['ff_b2'], 'L1_xattn_ln1_g': _L1_xattn_in['ln1_g'], 'L1_xattn_ln1_b': _L1_xattn_in['ln1_b'], 'L1_xattn_ln2_g': _L1_xattn_in['ln2_g'], 'L1_xattn_ln2_b': _L1_xattn_in['ln2_b'], 'L1_xattn_ln3_g': _L1_xattn_in['ln3_g'], 'L1_xattn_ln3_b': _L1_xattn_in['ln3_b']}

def reference(x, ctx_1024, mask_Bx1x1xS2_if1, mask_1x1xSxS_bk0, L0_xattn_wv, L0_xattn_wk, L0_xattn_wq, L0_xattn_w_out, L0_xattn_b_out, L0_xattn_g1, L0_xattn_beta1, L0_xattn_w_ff1, L0_xattn_b_ff1, L0_xattn_w_ff2, L0_xattn_b_ff2, L0_xattn_g2, L0_xattn_beta2, L1_xattn_sa_wq, L1_xattn_sa_bq, L1_xattn_sa_wk, L1_xattn_sa_bk, L1_xattn_sa_wv, L1_xattn_sa_bv, L1_xattn_sa_wo, L1_xattn_sa_bo, L1_xattn_ca_wq, L1_xattn_ca_bq, L1_xattn_ca_wk, L1_xattn_ca_bk, L1_xattn_ca_wv, L1_xattn_ca_bv, L1_xattn_ca_wo, L1_xattn_ca_bo, L1_xattn_ff_w1, L1_xattn_ff_b1, L1_xattn_ff_w2, L1_xattn_ff_b2, L1_xattn_ln1_g, L1_xattn_ln1_b, L1_xattn_ln2_g, L1_xattn_ln2_b, L1_xattn_ln3_g, L1_xattn_ln3_b):
    import jax
    import jax.numpy as jnp

    def _L0_xattn_ref(value, key, query, mask, wv, wk, wq, w_out, b_out, g1, beta1, w_ff1, b_ff1, w_ff2, b_ff2, g2, beta2):
        import jax, jax.numpy as jnp
        import numpy as np
        EMBED = 256
        HEADS = 16
        HEAD_DIM = EMBED // HEADS
        FF = 4 * EMBED
        EPS = 1e-05

        def layernorm(x, g, b):
            mu = jnp.mean(x, axis=-1, keepdims=True)
            var = jnp.mean((x - mu) ** 2, axis=-1, keepdims=True)
            return (x - mu) * jax.lax.rsqrt(var + EPS) * g + b
        B, S, E = query.shape
        v = value.reshape(B, -1, HEADS, HEAD_DIM) @ wv
        k = key.reshape(B, -1, HEADS, HEAD_DIM) @ wk
        q = query.reshape(B, -1, HEADS, HEAD_DIM) @ wq
        scores = jnp.einsum('bqhd,bkhd->bhqk', q, k)
        scores = jnp.where(mask == 0, jnp.float32(-1e+20), scores)
        attn = jax.nn.softmax(scores / jnp.sqrt(jnp.float32(EMBED)), axis=-1)
        out = jnp.einsum('bhqk,bkhd->bqhd', attn, v).reshape(B, S, E)
        attention = out @ w_out + b_out
        x = layernorm(attention + query, g1, beta1)
        ff = jax.nn.relu(x @ w_ff1 + b_ff1) @ w_ff2 + b_ff2
        return layernorm(ff + x, g2, beta2)

    def _L1_xattn_ref(x, encoder_outputs, tgt_mask, sa_wq, sa_bq, sa_wk, sa_bk, sa_wv, sa_bv, sa_wo, sa_bo, ca_wq, ca_bq, ca_wk, ca_bk, ca_wv, ca_bv, ca_wo, ca_bo, ff_w1, ff_b1, ff_w2, ff_b2, ln1_g, ln1_b, ln2_g, ln2_b, ln3_g, ln3_b):
        import jax, jax.numpy as jnp
        import numpy as np
        EMBED_DIM = 256
        NUM_HEADS = 16
        HEAD_DIM = EMBED_DIM // NUM_HEADS
        FF_DIM = 1024
        B, T, S = (2, 512, 512)
        LN_EPS = 1e-05

        def _layernorm(x, g, b):
            mu = jnp.mean(x, -1, keepdims=True)
            var = jnp.mean(jnp.square(x - mu), -1, keepdims=True)
            return (x - mu) * jax.lax.rsqrt(var + LN_EPS) * g + b

        def _mha(q_in, k_in, v_in, wq, bq, wk, bk, wv, bv, wo, bo, mask=None):
            Bq, Tq, C = q_in.shape
            Tk = k_in.shape[1]
            Q = (q_in @ wq + bq).reshape(Bq, Tq, NUM_HEADS, HEAD_DIM)
            K = (k_in @ wk + bk).reshape(Bq, Tk, NUM_HEADS, HEAD_DIM)
            V = (v_in @ wv + bv).reshape(Bq, Tk, NUM_HEADS, HEAD_DIM)
            scores = jnp.einsum('bqhd,bkhd->bhqk', Q, K) / np.sqrt(HEAD_DIM)
            if mask is not None:
                scores = jnp.where(mask, scores, -jnp.inf)
            attn = jax.nn.softmax(scores, axis=-1)
            out = jnp.einsum('bhqk,bkhd->bqhd', attn, V).reshape(Bq, Tq, C)
            return out @ wo + bo
        h = _layernorm(x, ln1_g, ln1_b)
        x = x + _mha(h, h, h, sa_wq, sa_bq, sa_wk, sa_bk, sa_wv, sa_bv, sa_wo, sa_bo, tgt_mask)
        h = _layernorm(x, ln2_g, ln2_b)
        x = x + _mha(h, encoder_outputs, encoder_outputs, ca_wq, ca_bq, ca_wk, ca_bk, ca_wv, ca_bv, ca_wo, ca_bo, None)
        h = _layernorm(x, ln3_g, ln3_b)
        ff = jax.nn.relu(h @ ff_w1 + ff_b1) @ ff_w2 + ff_b2
        return x + ff
    x = _L0_xattn_ref(ctx_1024, ctx_1024, x, mask_Bx1x1xS2_if1, L0_xattn_wv, L0_xattn_wk, L0_xattn_wq, L0_xattn_w_out, L0_xattn_b_out, L0_xattn_g1, L0_xattn_beta1, L0_xattn_w_ff1, L0_xattn_b_ff1, L0_xattn_w_ff2, L0_xattn_b_ff2, L0_xattn_g2, L0_xattn_beta2)
    x = _L1_xattn_ref(x, ctx_1024, mask_1x1xSxS_bk0, L1_xattn_sa_wq, L1_xattn_sa_bq, L1_xattn_sa_wk, L1_xattn_sa_bk, L1_xattn_sa_wv, L1_xattn_sa_bv, L1_xattn_sa_wo, L1_xattn_sa_bo, L1_xattn_ca_wq, L1_xattn_ca_bq, L1_xattn_ca_wk, L1_xattn_ca_bk, L1_xattn_ca_wv, L1_xattn_ca_bv, L1_xattn_ca_wo, L1_xattn_ca_bo, L1_xattn_ff_w1, L1_xattn_ff_b1, L1_xattn_ff_w2, L1_xattn_ff_b2, L1_xattn_ln1_g, L1_xattn_ln1_b, L1_xattn_ln2_g, L1_xattn_ln2_b, L1_xattn_ln3_g, L1_xattn_ln3_b)
    return x

_drawn_inputs = setup_inputs


def setup_inputs(seed=0):
    import zlib

    import numpy as np

    out = dict(_drawn_inputs(seed))
    spreads = {'L0_xattn_b_out': (0.0, 0.1),
     'L0_xattn_g1': (1.0, 0.2),
     'L0_xattn_beta1': (0.0, 0.1),
     'L0_xattn_b_ff1': (0.0, 0.1),
     'L0_xattn_b_ff2': (0.0, 0.1),
     'L0_xattn_g2': (1.0, 0.2),
     'L0_xattn_beta2': (0.0, 0.1),
     'L1_xattn_sa_bq': (0.0, 0.345),
     'L1_xattn_sa_bk': (0.0, 2.0),
     'L1_xattn_sa_bv': (0.0, 0.1),
     'L1_xattn_sa_bo': (0.0, 0.1),
     'L1_xattn_ca_bq': (0.0, 0.435),
     'L1_xattn_ca_bk': (0.0, 2.0),
     'L1_xattn_ca_bv': (0.0, 0.1),
     'L1_xattn_ca_bo': (0.0, 0.1),
     'L1_xattn_ff_b1': (0.0, 0.1),
     'L1_xattn_ff_b2': (0.0, 0.1),
     'L1_xattn_ln1_g': (1.0, 0.2),
     'L1_xattn_ln1_b': (0.0, 0.1),
     'L1_xattn_ln2_g': (1.0, 0.2),
     'L1_xattn_ln2_b': (0.0, 0.447),
     'L1_xattn_ln3_g': (1.0, 0.2),
     'L1_xattn_ln3_b': (0.0, 0.1)}
    factors = {'L0_xattn_wv': 3.928,
     'L0_xattn_wk': 48.818,
     'L0_xattn_wq': 50.355,
     'L0_xattn_w_out': 4.007}
    for name, (base, spread) in spreads.items():
        noise = np.random.default_rng([zlib.crc32(name.encode()), seed]).standard_normal(out[name].shape)
        drawn = base * np.exp(spread * noise) if base else spread * noise
        out[name] = jnp.asarray(drawn.astype(out[name].dtype))
    for name, factor in factors.items():
        out[name] = (out[name] * factor).astype(out[name].dtype)
    return out
```

```python
from contextlib import ExitStack

import concourse.bass as bass
from concourse import mybir

ALU = mybir.AluOpType
ACT = mybir.ActivationFunctionType
AX = mybir.AxisListType
F32 = mybir.dt.float32
F32R = mybir.dt.float32r
BF16 = mybir.dt.bfloat16
I32 = mybir.dt.int32
U8 = mybir.dt.uint8

P = 128
B, S, E = 16, 256, 256
H, HD = 16, 16
FF = 1024
LANES = 2
NI = B // LANES
FT = E // P
TT = S // P
NF = FF // P
HALVES, SLOTS = 2, 8
GROUPS = 4
HROWS = 64
R_MASK, R_A, R_B, R_C, R_MAX = 0, 1, 17, 33, 49
K_MAXPASS, K_EXPPASS = 49, 51
EPS = 1e-5
L0_MASKED = -1e20 / 16.0
L1_MASKED = -1e30
ROWS = ["g0", "be0", "g1", "be1", "g2", "be2", "g3", "be3", "g4", "be4",
        "b_res0", "b_ff0", "b_o1", "b_o2", "b_ff1", "bv1", "bv2"]
RI = {n: i for i, n in enumerate(ROWS)}
C_Q, C_K, C_F = 0, 4, 8
NCOLS = 8 + 2 * NF

SETUP_LOADS, SETUP_DMAS = 15, 25
SETUP_ACT = 2
SETUP_DVE_CHAIN = 17
SETUP_DVE = SETUP_DVE_CHAIN + 1


def merge(a, b, weight):
    total, out, i, done = sum(weight(x) for x in b) or 1, [], 0, 0.0
    for n, x in enumerate(a):
        out.append(x)
        while i < len(b) and done / total <= (n + 1) / len(a):
            done += weight(b[i])
            out.append(b[i])
            i += 1
    return out + b[i:]


def schedule():
    def enter(s):
        return [("load", 0, s), ("tc", 0, s), ("tx", 0, s), ("q", 0, s), ("r0", 0, s), ("stk", 0, s), ("stq", 0, s),
                ("v", 0, s)]

    def attend(l, s):
        def maxes(hs):
            return [("max", l, s, hs, t, sp, h) for t in range(TT) for sp in range(2) for h in range(HALVES)]

        def exps(g):
            return [("exp", l, s, g, kt, h) for kt in range(TT) for h in range(HALVES)]
        out = maxes(0) + [("nm", l, s, 0)] + maxes(1) + [("nm", l, s, 1)]
        for g in range(GROUPS):
            e = exps(g)
            out += e[:2] + ([("pv", l, s, g - 1)] if g else []) + e[2:]
        return out + [("pv", l, s, GROUPS - 1), ("oc", l, s)]

    def ffn(f, s):
        return [("ff1", f, s, c) for c in range(NF // 2)] + [("ff2", f, s)]

    def p1(s):
        return ([("o", 0, s), ("ln", 0, s), ("th", 0, s)] + ffn(0, s) + [("ln", 1, s), ("ln", 2, s), ("th", 1, s)]
                + [("r0", 1, s), ("k", 1, s), ("stk", 1, s), ("q", 1, s), ("stq", 1, s), ("v", 1, s)])

    def p2(s):
        return [("k", 2, s), ("stk", 2, s), ("v", 2, s), ("o", 1, s), ("ln", 3, s), ("th", 2, s), ("q", 2, s),
                ("stq", 2, s)]

    def p3(s):
        return [("o", 2, s), ("ln", 4, s), ("th", 3, s)] + ffn(1, s) + [("store", 0, s)]

    def weight(x):
        return {"load": 0, "r0": 0, "stq": 1, "stk": 1, "ln": 3, "ff1": 2, "ff2": 5, "store": 0}.get(x[0], 2)
    return (enter(0) + merge(attend(0, 0), enter(1), weight) + merge(attend(0, 1), p1(0), weight)
            + merge(attend(1, 0), p1(1), weight) + merge(attend(1, 1), p2(0), weight)
            + merge(attend(2, 0), p2(1), weight) + merge(attend(2, 1), p3(0), weight) + p3(1))


DENSE = ("tx", "tc", "q", "k", "nm", "o", "th", "ff1", "ff2")


def is_dense(x):
    return x[0] in DENSE or (x[0] == "v" and x[1] > 0)


class Signal:

    def __init__(self, sem, steps, inc):
        self.sem, self.inc = sem, inc
        self.order = {x: n + 1 for n, x in enumerate(steps)}
        self.per = inc * len(steps)

    def done(self, i, x, part=None):
        n = self.order[x] * self.inc
        if part is not None:
            n -= self.inc - part
        return i * self.per + (self.per + n)

    def ago(self, i, x, back=1):
        return i * self.per + (self.per + (self.order[x] - back) * self.inc)

    def last_iteration(self, i, x):
        return i * self.per + self.order[x] * self.inc


def build(nc, x, ctx_in, mask0, mask1, wq_rep, wk_rep, wv_rep, w_out, wqkv, wo, wff1, wff2, rows, cols, ident_in,
          same_slot, same_head, out, masks_dram):
    steps = schedule()
    dense = [s for s in steps if is_dense(s)]
    assert len(dense) % 2 == 0
    at = {s: n for n, s in enumerate(steps)}

    def of(*kinds):
        return [s for s in steps if s[0] in kinds]

    def before(pos, cand):
        ahead = [c for c in cand if at[c] < at[pos]]
        return (ahead[-1], True) if ahead else (cand[-1], False)

    with ExitStack() as ctx:
        def sb(name, shape, dt=F32):
            return ctx.enter_context(nc.sbuf_tensor(name, shape, dt))

        def sem(name):
            return ctx.enter_context(nc.semaphore(name))

        def signal(name, steps_, inc):
            return Signal(sem(name), steps_, inc)

        dense_ps = ctx.enter_context(nc.psum_tensor("dense_ps", [P, 2, 2, 256], F32))
        max_ps = ctx.enter_context(nc.psum_tensor("max_ps", [P, 2, 2, 256], F32))
        exp_ps = ctx.enter_context(nc.psum_tensor("exp_ps", [P, 2, 2, 256], F32))
        pv_ps = ctx.enter_context(nc.psum_tensor("pv_ps", [P, 2, 512], F32))

        qkv_w = sb("qkv_w", [P, 6, 2, FT, E], F32R)
        ff1_w = sb("ff1_w", [P, 2, 2, FT, FF], F32R)
        ff2_w = sb("ff2_w", [P, 2, NF, E])
        o_w = sb("o_w", [P, 3, FT, E])
        q0_w = sb("q0_w", [P, P])
        row = sb("row", [P, len(ROWS), E])
        col = sb("col", [P, NCOLS])
        ident = sb("ident", [P, P])
        ident_bf = sb("ident_bf", [P, P], BF16)
        bias_qk = sb("bias_qk", [P, TT, S], BF16)
        bias_kq = sb("bias_kq", [P, TT, S], BF16)
        nan_col = sb("nan_col", [P, TT])
        minus_half = sb("minus_half", [P, TT])
        gate = sb("gate", [P, 2])

        x_tok = sb("x_tok", [P, TT, E])
        ctx_tok = sb("ctx_tok", [P, TT, E])
        ctxT = sb("ctxT", [P, LANES, 2, FT, S], F32R)
        qT = sb("qT", [P, 2, FT, S], F32R)
        kT = sb("kT", [P, 2, FT, S], F32R)
        q_stack = sb("q_stack", [P, LANES, SLOTS, S], F32R)
        k_stack = sb("k_stack", [P, LANES, SLOTS, S], F32R)
        v_ones = sb("v_ones", [P, LANES, TT, H, 2 * HD])
        m_tok = sb("m_tok", [P, 2, TT, 8])
        nm_tok = sb("nm_tok", [P, 2, TT, P])
        nmT = sb("nmT", [16, 2, S], F32R)
        probs = sb("probs", [P, 2, HALVES * TT * 2, S])
        den = sb("den", [P, 2, S])
        attn_pad = sb("attn_pad", [P, GROUPS, S])
        attn = sb("attn", [P, FT, S])
        res = sb("res", [P, LANES, TT, E])
        y = sb("y", [P, TT, E])
        z = sb("z", [P, TT, E])
        hx = sb("hx", [P, TT, E])
        hT = sb("hT", [P, 2, FT, S], F32R)
        hid = sb("hid", [P, NF, S])
        xT = hid[:, 0:FT, :]
        st = sb("st", [P, TT, 6])
        mv = sb("mv", [P, TT, 2])
        rstd = sb("rstd", [P, TT])
        vare = sb("vare", [P, TT])

        loaded = [signal(f"loaded{s}", [("load", 0, s)], 32) for s in range(LANES)]
        dense_full = signal("dense_full", dense, 1)
        evacuated = [signal(f"evacuated{b}", dense[b::2], 2) for b in range(2)]
        pool_v = signal("pool_v", [("v", 0, s) for s in range(LANES)], 1)
        q_stacked = [signal(f"q_stacked{s}", [e for e in of("stq") if e[2] == s], 96) for s in range(LANES)]
        k_stacked = [signal(f"k_stacked{s}", [e for e in of("stk") if e[2] == s], 96) for s in range(LANES)]
        mask_row = [signal(f"mask_row{s}", [e for e in of("r0") if e[2] == s], 32) for s in range(LANES)]
        max_full = signal("max_full", of("max"), 1)
        max_taken = signal("max_taken", of("max"), 1)
        neg_hi = signal("neg_hi", of("nm"), 2)
        neg_lo = signal("neg_lo", of("nm"), 1)
        max_rows = [signal(f"max_rows{hs}", [e for e in of("nm") if e[3] == hs], 32) for hs in range(2)]
        exp_full = signal("exp_full", of("exp"), 1)
        probs_ready = signal("probs_ready", of("exp"), 1)
        pv_full = signal("pv_full", of("pv"), 1)
        den_spread = signal("den_spread", of("pv"), 1)
        den_inverse = signal("den_inverse", of("pv"), 1)
        normed = signal("normed", of("pv"), 1)
        compacted = signal("compacted", of("oc"), 64)
        stats_part = signal("stats_part", of("ln"), 1)
        stats = signal("stats", of("ln"), 1)
        eps_added = signal("eps_added", of("ln"), 1)
        rstd_ready = signal("rstd_ready", of("ln"), 1)
        scaled = signal("scaled", of("ln"), 1)
        ln_done = signal("ln_done", of("ln"), 1)
        res_steps = [s for s in steps if s[0] == "v" and s[1] == 0 or s[0] == "ln" and s[1] != 2]
        res_ready = signal("res_ready", res_steps, 1)
        stored = signal("stored", of("store"), 16)
        every = [*loaded, dense_full, *evacuated, pool_v, *q_stacked, *k_stacked, *mask_row, max_full, max_taken, neg_hi, neg_lo,
                 *max_rows, exp_full, probs_ready, pv_full, den_spread, den_inverse, normed, compacted, stats_part,
                 stats, eps_added, rstd_ready, scaled, ln_done, res_ready, stored]

        primed = sem("primed")
        s_const = sem("s_const")
        s_raw = [sem("s_raw0"), sem("s_raw1")]
        s_hi = sem("s_hi")
        s_lo = sem("s_lo")
        s_dve = sem("s_dve")
        s_pe = sem("s_pe")
        s_act = sem("s_act")
        carrier = sem("carrier")
        carrier_sp = sem("carrier_sp")
        carrier_dve = sem("carrier_dve")

        block = ctx.enter_context(nc.Block())

        bank = {s: n % 2 for n, s in enumerate(dense)}

        def prev(sig, i, pos, cand):
            s, here = before(pos, cand)
            return sig.done(i, s) if here else sig.last_iteration(i, s)

        stage = probs[:].rearrange("p a b e -> p a (b e)")

        splits = []
        for n in range(6):
            splits.append((qkv_w[:, n, 0].rearrange("p k e -> p (k e)"), qkv_w[:, n, 1].rearrange("p k e -> p (k e)"),
                           wqkv[n], FT, 0.25 if n % 3 == 0 else 1.0))
        for f in range(2):
            splits.append((ff1_w[:, f, 0].rearrange("p k e -> p (k e)"), ff1_w[:, f, 1].rearrange("p k e -> p (k e)"),
                           wff1[f], FT, 1.0))

        @block.sync
        def _(sp):
            sp.dma_start(ident[:], ident_in).then_inc(s_const, 16)
            sp.dma_start(row[:].rearrange("p r e -> p (r e)"),
                         rows.partition_broadcast(P)).then_inc(s_const, 16)
            sp.dma_start(col[:], cols).then_inc(s_const, 16)
            sp.dma_start(y[:, 0, 0:P], same_slot).then_inc(s_const, 16)
            sp.dma_start(y[:, 0, P:2 * P], same_head).then_inc(s_const, 16)
            sp.dma_start(y[:, 1, 0:P], wv_rep).then_inc(s_const, 16)
            sp.dma_start(z[0:HD, 0, 0:P], wq_rep).then_inc(s_const, 16)
            sp.dma_start(z[0:HD, 0, P:2 * P], wk_rep).then_inc(s_const, 16)
            sp.dma_start(hx[0:B, 0, :].bitcast(I32), mask0).then_inc(s_const, 16)
            sp.dma_start(x_tok[:, :, 0:S // 4].bitcast(I32), mask1.rearrange("(t p) k -> p t k", p=P)).then_inc(s_const, 16)
            sp.dma_start(attn[:], w_out.rearrange("(t p) e -> p t e", p=P)).then_inc(s_const, 16)
            for l in range(2):
                sp.dma_start(o_w[:, l + 1], wo[l].rearrange("(t p) e -> p t e", p=P)).then_inc(s_const, 16)
                sp.dma_start(ff2_w[:, l], wff2[l].rearrange("(t p) e -> p t e", p=P)).then_inc(s_const, 16)
            for n, (_, _, src, k, _) in enumerate(splits):
                if n >= 2:
                    sp.wait_ge(s_lo, n - 1)
                w = k * src.shape[1]
                sp.dma_start(stage[:, n % 2, 0:w].rearrange("p (t e) -> p t e", t=k),
                             src.rearrange("(t p) e -> p t e", p=P)).then_inc(s_raw[n % 2], 16)
            sp.wait_ge(s_dve, 7)
            sp.dma_start(masks_dram[0:B], hx[0:B, 1, :]).then_inc(s_const, 16)
            sp.dma_start(masks_dram[B:B + 1], z[0:1, 1, :]).then_inc(s_const, 16)
            for s in range(LANES):
                for h in range(HALVES):
                    sp.dma_start(q_stack[HROWS * h:HROWS * h + 1, s].bitcast(F32), hid[0:1, 0:SLOTS, :]).then_inc(s_const, 16)
                    sp.dma_start(k_stack[HROWS * h + R_MAX:HROWS * h + R_MAX + 2, s].bitcast(F32),
                                 hid[0:2, 0:SLOTS, :]).then_inc(s_const, 16)
            sp.wait_ge(s_const, 16 * SETUP_DMAS)
            sp.wait_ge(primed, 1)
            sp.wait_ge(s_act, SETUP_ACT)
            sp.wait_ge(s_dve, SETUP_DVE)

            def wait(sg, value):
                sp.wait_ge(sg.sem, value)
                sp.sem_inc(carrier_sp, 1)

            with sp.Fori(0, NI) as i:
                for step in steps:
                    kind, l, s = step[:3]
                    if kind == "load":
                        wait(dense_full, prev(dense_full, i, step, of("tx")))
                        wait(pool_v, prev(pool_v, i, step, [("v", 0, 0), ("v", 0, 1)]))
                        wait(res_ready, prev(res_ready, i, step, [("v", 0, 0), ("v", 0, 1)]))
                        b = i * LANES + s
                        sp.dma_start(ctx_tok[:], ctx_in[bass.ds(b, 1)].rearrange("a (t p) e -> p (a t) e", p=P)
                                     ).then_inc(loaded[s].sem, 16)
                        sp.dma_start(x_tok[:], x[bass.ds(b, 1)].rearrange("a (t p) e -> p (a t) e", p=P)
                                     ).then_inc(loaded[s].sem, 16)
                    elif kind == "r0":
                        wait(exp_full, prev(exp_full, i, step, [e for e in of("exp") if e[2] == s]))
                        src = masks_dram[bass.ds(i * LANES + s, 1)] if l == 0 else masks_dram[B:B + 1]
                        for h in range(HALVES):
                            sp.dma_start(k_stack[HROWS * h:HROWS * h + 1, s].bitcast(F32),
                                         src.rearrange("a (o k) -> a o k", o=1).to_broadcast([1, SLOTS, S])
                                         ).then_inc(mask_row[s].sem, 16)
                    elif kind in ("stq", "stk"):
                        key = ("q" if kind == "stq" else "k", l, s)
                        if kind == "stk" and l == 0:
                            key = ("tc", 0, s)
                        wait(evacuated[bank[key]], evacuated[bank[key]].done(i, key))
                        wait(exp_full, prev(exp_full, i, step, [e for e in of("exp") if e[2] == s]))
                        sg = (q_stacked if kind == "stq" else k_stacked)[s]
                        dst, parts = (q_stack, (0, 0, 1)) if kind == "stq" else (k_stack, (0, 1, 0))
                        for r, part in zip((R_A, R_B, R_C), parts):
                            for h in range(HALVES):
                                src = (qT if kind == "stq" else kT)[:, part, h, :]
                                if kind == "stk" and l == 0:
                                    src = ctxT[:, s, part, h, :]
                                sp.dma_start(dst[HROWS * h + r:HROWS * h + r + HD, s].bitcast(F32), src.bitcast(F32)
                                             ).then_inc(sg.sem, 16)
                    elif kind == "nm":
                        hs = step[3]
                        wait(evacuated[bank[step]], evacuated[bank[step]].done(i, step))
                        wait(exp_full, prev(exp_full, i, step, [e for e in of("exp") if e[2] == s and
                                                                          e[3] // 2 == hs]))
                        for h in range(HALVES):
                            sp.dma_start(q_stack[HROWS * h + R_MAX:HROWS * h + R_MAX + 2, s, 4 * hs:4 * hs + 4
                                                 ].bitcast(F32),
                                         nmT[8 * h:8 * h + 8, hs, :].bitcast(F32)).then_inc(max_rows[hs].sem, 16)
                    elif kind == "oc":
                        wait(normed, normed.done(i, ("pv", l, s, GROUPS - 1)))
                        wait(dense_full, prev(dense_full, i, step, of("o")))
                        for j in range(4):
                            sp.dma_start(attn[64 * (j % 2):64 * (j % 2) + 64, j // 2, :],
                                         attn_pad[32 * j:32 * j + HD]).then_inc(compacted.sem, 16)
                    elif kind == "store":
                        key = ("ff2", 1, s)
                        wait(evacuated[bank[key]], evacuated[bank[key]].done(i, key))
                        b = i * LANES + s
                        sp.dma_start(out[bass.ds(b, 1)].rearrange("a (t p) e -> p (a t) e", p=P), y[:]
                                     ).then_inc(stored.sem, 16)
            sp.wait_ge(stored.sem, stored.per * (NI + 1))

        @block.gpsimd
        def _(pool):
            for sg in every:
                pool.sem_inc(sg.sem, sg.per)
            pool.sem_inc(primed, 1)
            pool.wait_ge(s_act, SETUP_ACT)
            pool.wait_ge(s_dve, SETUP_DVE)
            pool.wait_ge(s_const, 16 * SETUP_DMAS)

            def wait(sg, value):
                pool.wait_ge(sg.sem, value)

            def hold():
                pool.sem_inc(carrier, 1)

            with pool.Fori(0, NI) as i:
                for step in steps:
                    kind, l, s = step[:3]
                    if kind == "v" and l == 0:
                        wait(loaded[s], loaded[s].done(i, ("load", 0, s)))
                        hold()
                        wait(pv_full, prev(pv_full, i, step, [e for e in of("pv") if e[2] == s]))
                        hold()
                        for t in range(TT):
                            for h in range(HALVES):
                                last = nc.gpsimd.tensor_copy(
                                    v_ones[:, s, t, SLOTS * h:SLOTS * h + SLOTS, 0:HD],
                                    ctx_tok[:, t, P * h:P * h + P].rearrange("p (d s) -> p s d", d=HD))
                        last.then_inc(pool_v.sem, 1)
                        wait(evacuated[bank[("o", 2, s)]],
                             prev(evacuated[bank[("o", 2, s)]], i, step, [("o", 2, s)]))
                        hold()
                        wait(evacuated[bank[("ff2", 1, s)]],
                             prev(evacuated[bank[("ff2", 1, s)]], i, step, [("ff2", 1, s)]))
                        hold()
                        for t in range(TT):
                            last = nc.gpsimd.tensor_tensor(res[:, s, t], x_tok[:, t], row[:, RI["b_res0"]], ALU.add)
                        last.then_inc(res_ready.sem, 1)
                    elif kind == "ln":
                        n = l
                        wait(stats, stats.done(i, step))
                        hold()
                        nc.gpsimd.tensor_scalar(vare[:], mv[:, :, 1], EPS, None, ALU.add).then_inc(eps_added.sem, 1)
                        wait(eps_added, eps_added.done(i, step))
                        nc.gpsimd.tensor_tensor(rstd[:], vare[:], minus_half[:], ALU.pow).then_inc(rstd_ready.sem, 1)
                        if n == 2:
                            continue
                        if n < 2:
                            wait(ln_done, ln_done.done(i, step))
                        else:
                            key = ("o", n - 2, s)
                            wait(evacuated[bank[key]], evacuated[bank[key]].done(i, key))
                        hold()
                        src = hx if n == 0 else y
                        b = {0: "b_ff0", 1: "b_o1", 3: "b_o2", 4: "b_ff1"}[n]
                        for t in range(TT):
                            last = nc.gpsimd.tensor_tensor(res[:, s, t], src[:, t], row[:, RI[b]], ALU.add)
                        last.then_inc(res_ready.sem, 1)

        @block.scalar
        def _(act):
            for n, (hi, _, src, k, scale) in enumerate(splits):
                act.wait_ge(s_raw[n % 2], 16 * (n // 2 + 1))
                nc.scalar.activation(hi, stage[:, n % 2, 0:k * src.shape[1]], ACT.Copy, scale=scale).then_inc(s_hi, 1)
            act.wait_ge(s_pe, 1)
            nc.scalar.activation(o_w[:, 0], dense_ps[:, 1], ACT.Copy).then_inc(s_act, 1)
            act.wait_ge(s_pe, 2)
            nc.scalar.activation(bias_kq[:], max_ps[:, 0], ACT.Copy).then_inc(s_act, 1)
            act.wait_ge(primed, 1)
            act.wait_ge(s_dve, SETUP_DVE)

            def full(i, step):
                act.wait_ge(dense_full.sem, dense_full.done(i, step))

            with act.Fori(0, NI) as i:
                for step in steps:
                    kind, l, s = step[:3]
                    d = dense_ps[:, bank[step]] if step in bank else None
                    ev = evacuated[bank[step]].sem if step in bank else None
                    if kind == "tc":
                        full(i, step)
                        act.wait_ge(k_stacked[s].sem, k_stacked[s].last_iteration(i, ("stk", 0, s)))
                        nc.scalar.activation(ctxT[:, s, 0], d, ACT.Copy).then_inc(ev, 1)
                    elif kind == "tx":
                        full(i, step)
                        nc.scalar.activation(xT, d, ACT.Copy).then_inc(ev, 2)
                    elif kind in ("q", "k"):
                        full(i, step)
                        for sg, st_kind in ((q_stacked, "stq"),) if kind == "q" else ((k_stacked, "stk"),):
                            for lane in range(LANES):
                                act.wait_ge(sg[lane].sem, prev(sg[lane], i, step,
                                                               [e for e in of(st_kind) if e[2] == lane
                                                                and (kind == "q" or e[1] > 0)]))
                        dst = (qT if kind == "q" else kT)
                        if l == 0:
                            nc.scalar.activation(dst[:, 0], d, ACT.Copy).then_inc(ev, 1)
                        else:
                            c = (C_Q if kind == "q" else C_K) + (l - 1) * FT
                            for f in range(FT):
                                last = nc.scalar.activation(dst[:, 0, f], d[:, f], ACT.Identity,
                                                            bias=col[:, c + f:c + f + 1])
                            last.then_inc(ev, 1)
                    elif kind == "nm":
                        full(i, step)
                        act.wait_ge(max_rows[step[3]].sem, max_rows[step[3]].ago(i, step))
                        nc.scalar.activation(nmT[:, step[3]], d.rearrange("p a q -> p (a q)")[0:16, 0:S], ACT.Copy
                                             ).then_inc(ev, 2)
                    elif kind == "th":
                        full(i, step)
                        nc.scalar.activation(hT[:, 0], d, ACT.Copy).then_inc(ev, 1)
                    elif kind == "ff1":
                        full(i, step)
                        for f in range(2):
                            m = 2 * step[3] + f
                            c = C_F + l * NF + m
                            last = nc.scalar.activation(hid[:, m], d[:, f], ACT.Relu, bias=col[:, c:c + 1])
                        last.then_inc(ev, 2)
                    elif kind == "exp":
                        g, kt, h = step[3:]
                        act.wait_ge(exp_full.sem, exp_full.done(i, step))
                        if kt == 0 and h == 0:
                            act.wait_ge(pv_full.sem, pv_full.ago(i, ("pv", l, s, g), 2))
                        n = exp_full.order[step] - 1
                        nc.scalar.activation(probs[:, g % 2, 4 * h + 2 * kt:4 * h + 2 * kt + 2], exp_ps[:, n % 2], ACT.Exp
                                             ).then_inc(probs_ready.sem, 1)

        @block.vector
        def _(dve):
            waits = [0]

            def chain(ins):
                waits[0] += 1
                ins.then_inc(s_dve, 1)
                dve.wait_ge(s_dve, waits[0])
            chain(nc.vector.memset(hid[:], 1.0))
            chain(nc.vector.memset(v_ones[:], 1.0))
            chain(nc.vector.memset(nm_tok[:], 0.0))
            chain(nc.vector.memset(minus_half[:], -0.5))
            chain(nc.vector.memset(z[0:1, 1, :], 0.0))
            dve.wait_ge(s_const, 16 * SETUP_LOADS)
            chain(nc.vector.tensor_copy(hx[0:B, 1, :], hx[0:B, 0, :].bitcast(I32)))
            chain(nc.vector.tensor_scalar(hx[0:B, 1, :].bitcast(F32R), hx[0:B, 1, :], 0.0, L0_MASKED,
                                          ALU.is_equal, ALU.mult))
            chain(nc.vector.tensor_copy(ctx_tok[:], x_tok[:].bitcast(U8)[:, :, 0:S]))
            chain(nc.vector.tensor_scalar(ctx_tok[:], ctx_tok[:], 0.0, L1_MASKED, ALU.is_equal, ALU.mult))
            chain(nc.vector.tensor_copy(bias_qk[:], ctx_tok[:]))
            chain(nc.vector.tensor_copy(ident_bf[:], ident[:]))
            chain(nc.vector.tensor_reduce(nan_col[:], ctx_tok[:], AX.X, ALU.max))
            chain(nc.vector.tensor_scalar(nan_col[:], nan_col[:], 1e30, None, ALU.mult))
            chain(nc.vector.tensor_tensor(nan_col[:], nan_col[:], nan_col[:], ALU.subtract))
            chain(nc.vector.tensor_scalar(col[:, C_Q:C_Q + 4], col[:, C_Q:C_Q + 4], 0.25, None, ALU.mult))
            chain(nc.vector.tensor_tensor(y[:, 1, 0:P], y[:, 1, 0:P], y[:, 0, P:2 * P], ALU.mult))
            dve.wait_ge(s_pe, 1)
            chain(nc.vector.scalar_tensor_tensor(q0_w[:], dense_ps[:, 0, 0, 0:P], 1.0 / 16.0, y[:, 0, 0:P],
                                                 ALU.mult, ALU.mult))
            assert waits[0] == SETUP_DVE_CHAIN, waits[0]
            for n, (hi, lo, src, k, scale) in enumerate(splits):
                dve.wait_ge(s_hi, n + 1)
                nc.vector.scalar_tensor_tensor(lo, stage[:, n % 2, 0:k * src.shape[1]], scale, hi.bitcast(F32),
                                               ALU.mult, ALU.subtract).then_inc(s_lo, 1)
            dve.wait_ge(s_lo, len(splits))
            nc.vector.memset(gate[:], 0.0).then_inc(s_dve, 1)
            dve.wait_ge(s_act, SETUP_ACT)
            dve.wait_ge(primed, 1)
            dve.wait_ge(s_const, 16 * SETUP_DMAS)

            def full(i, step):
                dve.wait_ge(dense_full.sem, dense_full.done(i, step))

            def hold():
                nc.vector.memset(gate[:, 0:1], 0.0)

            with dve.Fori(0, NI) as i:
                for step in steps:
                    kind, l, s = step[:3]
                    d = dense_ps[:, bank[step]] if step in bank else None
                    ev = evacuated[bank[step]] if step in bank else None
                    if kind == "tc":
                        dve.wait_ge(ev.sem, ev.done(i, step, 1))
                        nc.vector.tensor_tensor(ctxT[:, s, 1], d, ctxT[:, s, 0].bitcast(F32), ALU.subtract
                                                ).then_inc(ev.sem, 1)
                    elif kind in ("q", "k"):
                        dve.wait_ge(ev.sem, ev.done(i, step, 1))
                        dst = qT if kind == "q" else kT
                        if l == 0:
                            nc.vector.tensor_tensor(dst[:, 1], d, dst[:, 0].bitcast(F32), ALU.subtract
                                                    ).then_inc(ev.sem, 1)
                        else:
                            c = (C_Q if kind == "q" else C_K) + (l - 1) * FT
                            for f in range(FT):
                                last = nc.vector.scalar_tensor_tensor(dst[:, 1, f], d[:, f], col[:, c + f:c + f + 1],
                                                                      dst[:, 0, f].bitcast(F32), ALU.add,
                                                                      ALU.subtract)
                            last.then_inc(ev.sem, 1)
                    elif kind == "th":
                        dve.wait_ge(ev.sem, ev.done(i, step, 1))
                        nc.vector.tensor_tensor(hT[:, 1], d, hT[:, 0].bitcast(F32), ALU.subtract).then_inc(ev.sem, 1)
                    elif kind == "v" and l > 0:
                        full(i, step)
                        for t in range(TT):
                            last = nc.vector.tensor_tensor(
                                v_ones[:, s, t, :, 0:HD], d[:, t].rearrange("p (h e) -> p h e", h=H),
                                row[:, RI[f"bv{l}"]].rearrange("p (h e) -> p h e", h=H), ALU.add)
                        last.then_inc(ev.sem, 2)
                    elif kind == "max":
                        hs, t, sp_, h = step[3:]
                        dve.wait_ge(max_full.sem, max_full.done(i, step))
                        if t == 0 and sp_ == 0 and h == 0:
                            dve.wait_ge(neg_lo.sem, prev(neg_lo, i, step, [e for e in of("nm") if e[3] == hs]))
                        n = max_full.order[step] - 1
                        c = 4 * h + 2 * sp_
                        nc.vector.tensor_reduce(m_tok[:, hs, t, c:c + 2], max_ps[:, n % 2], AX.X, ALU.max
                                                ).then_inc(max_taken.sem, 1)
                    elif kind == "nm":
                        hs = step[3]
                        last_max = ("max", l, s, hs, TT - 1, 1, HALVES - 1)
                        dve.wait_ge(max_taken.sem, max_taken.done(i, last_max))
                        dve.wait_ge(dense_full.sem, prev(dense_full, i, step, [e for e in of("nm") if e[3] == hs]))
                        for t in range(TT):
                            v4 = nm_tok[:, hs, t, 0:16].rearrange("p (h c k) -> p c h k", h=2, c=2)
                            m4 = m_tok[:, hs, t].rearrange("p (h k) -> p h k", h=2)
                            hi = v4[:, 0].bitcast(F32R)
                            if l == 1:
                                ins = nc.vector.tensor_scalar(hi, m4, -1.0, nan_col[:, t:t + 1], ALU.mult, ALU.add)
                            else:
                                ins = nc.vector.tensor_scalar(hi, m4, -1.0, None, ALU.mult)
                            ins.then_inc(neg_hi.sem, 1)
                        dve.wait_ge(neg_hi.sem, neg_hi.done(i, step))
                        for t in range(TT):
                            v4 = nm_tok[:, hs, t, 0:16].rearrange("p (h c k) -> p c h k", h=2, c=2)
                            m4 = m_tok[:, hs, t].rearrange("p (h k) -> p h k", h=2)
                            last = nc.vector.scalar_tensor_tensor(v4[:, 1], m4, -1.0, v4[:, 0], ALU.mult,
                                                                  ALU.subtract)
                        last.then_inc(neg_lo.sem, 1)
                    elif kind == "pv":
                        g = step[3]
                        n = pv_full.order[step] - 1
                        dve.wait_ge(pv_full.sem, pv_full.done(i, step))
                        hold()
                        nc.vector.stream_shuffle(den[:, n % 2], pv_ps[:, n % 2, 0:S],
                                                 [HD + k % HD for k in range(32)]).then_inc(den_spread.sem, 1)
                        dve.wait_ge(den_spread.sem, den_spread.done(i, step))
                        nc.vector.reciprocal(den[:, n % 2], den[:, n % 2]).then_inc(den_inverse.sem, 1)
                        dve.wait_ge(den_inverse.sem, den_inverse.done(i, step))
                        if g == 0:
                            dve.wait_ge(compacted.sem, prev(compacted, i, step, of("oc")))
                        nc.vector.tensor_tensor(attn_pad[:, g], pv_ps[:, n % 2, 0:S], den[:, n % 2], ALU.mult
                                                ).then_inc(normed.sem, 1)
                    elif kind == "o" or kind == "ff2":
                        full(i, step)
                        key = {("o", 0): ("v", 0, s), ("ff2", 0): ("ln", 0, s), ("o", 1): ("ln", 1, s),
                               ("o", 2): ("ln", 3, s), ("ff2", 1): ("ln", 4, s)}[kind, l]
                        dve.wait_ge(res_ready.sem, res_ready.done(i, key))
                        if kind == "o":
                            dve.wait_ge(stored.sem, prev(stored, i, step, of("store")))
                            dve.wait_ge(res_ready.sem, prev(res_ready, i, step, res_steps))
                        nc.vector.tensor_tensor(y[:], d, res[:, s], ALU.add).then_inc(ev.sem, 2)
                    elif kind == "ln":
                        n = l
                        src = {0: ("o", 0, s), 1: ("ff2", 0, s), 2: ("ln", 1, s), 3: ("o", 1, s), 4: ("o", 2, s)}[n]
                        if n == 2:
                            dve.wait_ge(ln_done.sem, ln_done.done(i, src))
                        else:
                            dve.wait_ge(evacuated[bank[src]].sem, evacuated[bank[src]].done(i, src))
                        for t in range(TT):
                            last = nc.vector.bn_stats(st[:, t], y[:, t])
                        last.then_inc(stats_part.sem, 1)
                        dve.wait_ge(stats_part.sem, stats_part.done(i, step))
                        dve.wait_ge(eps_added.sem, eps_added.ago(i, step))
                        hold()
                        for t in range(TT):
                            last = nc.vector.bn_aggr(mv[:, t], st[:, t])
                        last.then_inc(stats.sem, 1)
                        dve.wait_ge(stats.sem, stats.done(i, step))
                        for t in range(TT):
                            last = nc.vector.scalar_tensor_tensor(z[:, t], y[:, t], mv[:, t, 0:1], row[:, RI[f"g{n}"]],
                                                                  ALU.subtract, ALU.mult)
                        last.then_inc(scaled.sem, 1)
                        dve.wait_ge(scaled.sem, scaled.done(i, step))
                        dve.wait_ge(rstd_ready.sem, rstd_ready.done(i, step))
                        if n != 1:
                            dve.sem_inc(carrier_dve, 1)
                            dve.wait_ge(dense_full.sem, prev(dense_full, i, step, of("th")))
                            dve.sem_inc(carrier_dve, 1)
                            dve.wait_ge(res_ready.sem, prev(res_ready, i, step,
                                                            [e for e in res_steps if e[0] == "ln" and e[1] == 0]))
                        dst = y if n == 1 else hx
                        for t in range(TT):
                            last = nc.vector.scalar_tensor_tensor(dst[:, t], z[:, t], rstd[:, t:t + 1],
                                                                  row[:, RI[f"be{n}"]], ALU.mult, ALU.add)
                        last.then_inc(ln_done.sem, 1)

        @block.tensor
        def _(pe):
            pe.wait_ge(s_const, 16 * SETUP_LOADS)
            pe.wait_ge(s_dve, SETUP_DVE_CHAIN - 1)
            nc.tensor.matmul(dense_ps[:, 0, 0, 0:P], z[0:HD, 0, 0:P], z[0:HD, 0, P:2 * P], start=True, stop=True)
            for t in range(FT):
                last = nc.tensor.matmul(dense_ps[:, 1, t], y[:, 1, 0:P], attn[:, t], start=True, stop=True)
            last.then_inc(s_pe, 1)
            for kt in range(TT):
                for t in range(TT):
                    last = nc.tensor.transpose(max_ps[:, 0, kt, P * t:P * t + P], ctx_tok[:, t, P * kt:P * kt + P],
                                               ident[:])
            last.then_inc(s_pe, 1)
            pe.wait_ge(s_act, SETUP_ACT)
            pe.wait_ge(s_dve, SETUP_DVE)
            pe.wait_ge(s_const, 16 * SETUP_DMAS)
            pe.wait_ge(primed, 1)

            def free(i, step):
                ev = evacuated[bank[step]]
                pe.wait_ge(ev.sem, ev.ago(i, step))

            def ready(i, key):
                pe.wait_ge(evacuated[bank[key]].sem, evacuated[bank[key]].done(i, key))

            def split_product(ps, w, mov, kts):
                parts = [(0, 0), (1, 0), (0, 1)]
                for n, (a, b) in enumerate(parts):
                    for k in range(kts):
                        mm = nc.tensor.matmul(ps, w(a, k), mov(b, k), start=(n == 0 and k == 0),
                                              stop=(n == 2 and k == kts - 1))
                return mm

            with pe.Fori(0, NI) as i:
                for step in steps:
                    kind, l, s = step[:3]
                    d = dense_ps[:, bank[step]] if step in bank else None
                    if kind in ("tc", "tx", "th"):
                        if kind == "th":
                            key = ("ln", {0: 0, 1: 2, 2: 3, 3: 4}[l], s)
                            pe.wait_ge(ln_done.sem, ln_done.done(i, key))
                            src = hx
                        else:
                            pe.wait_ge(loaded[s].sem, loaded[s].done(i, ("load", 0, s)))
                            src = ctx_tok if kind == "tc" else x_tok
                        free(i, step)
                        for f in range(FT):
                            for t in range(TT):
                                mm = nc.tensor.transpose(d[:, f, P * t:P * t + P], src[:, t, P * f:P * f + P],
                                                         ident[:])
                        mm.then_inc(dense_full.sem, 1)
                    elif kind == "q" and l == 0:
                        ready(i, ("tx", 0, s))
                        free(i, step)
                        for f in range(FT):
                            mm = nc.tensor.matmul(d[:, f], q0_w[:], xT[:, f], start=True, stop=True)
                        mm.then_inc(dense_full.sem, 1)
                    elif kind in ("q", "k"):
                        w = 3 * (l - 1) + (kind == "k")
                        own = kind == "q" or l == 1
                        ready(i, ("th", l, s) if own else ("tc", 0, s))
                        free(i, step)
                        for f in range(FT):
                            mm = split_product(d[:, f], lambda a, k: qkv_w[:, w, a, k, P * f:P * f + P],
                                               lambda b, k: hT[:, b, k] if own else ctxT[:, s, b, k], FT)
                        mm.then_inc(dense_full.sem, 1)
                    elif kind == "v" and l > 0:
                        w = 3 * (l - 1) + 2
                        src = hT if l == 1 else ctxT[:, s]
                        free(i, step)
                        for t in range(TT):
                            mm = split_product(d[:, t], lambda a, k: src[:, a, k, P * t:P * t + P],
                                               lambda b, k: qkv_w[:, w, b, k], FT)
                        mm.then_inc(dense_full.sem, 1)
                    elif kind == "nm":
                        hs = step[3]
                        pe.wait_ge(neg_lo.sem, neg_lo.done(i, step))
                        free(i, step)
                        dd = d.rearrange("p a q -> p (a q)")
                        for t in range(TT):
                            mm = nc.tensor.transpose(dd[:, P * t:P * t + P], nm_tok[:, hs, t], ident[:])
                        mm.then_inc(dense_full.sem, 1)
                    elif kind == "o":
                        pe.wait_ge(compacted.sem, compacted.done(i, ("oc", l, s)))
                        free(i, step)
                        for t in range(TT):
                            for k in range(FT):
                                mm = nc.tensor.matmul(d[:, t], attn[:, k, P * t:P * t + P], o_w[:, l, k],
                                                      start=(k == 0), stop=(k == FT - 1))
                        mm.then_inc(dense_full.sem, 1)
                    elif kind == "ff1":
                        if step[3] == 0:
                            ready(i, ("th", 0 if l == 0 else 3, s))
                        free(i, step)
                        for f in range(2):
                            m = 2 * step[3] + f
                            mm = split_product(d[:, f], lambda a, k: ff1_w[:, l, a, k, P * m:P * m + P],
                                               lambda b, k: hT[:, b, k], FT)
                        mm.then_inc(dense_full.sem, 1)
                    elif kind == "ff2":
                        ready(i, ("ff1", l, s, NF // 2 - 1))
                        ready(i, ("ff1", l, s, NF // 2 - 2))
                        free(i, step)
                        for t in range(TT):
                            for k in range(NF):
                                mm = nc.tensor.matmul(d[:, t], hid[:, k, P * t:P * t + P], ff2_w[:, l, k],
                                                      start=(k == 0), stop=(k == NF - 1))
                        mm.then_inc(dense_full.sem, 1)
                    elif kind == "max":
                        hs, t, sp_, h = step[3:]
                        if hs == 0 and t == 0 and sp_ == 0 and h == 0:
                            pe.wait_ge(q_stacked[s].sem, q_stacked[s].done(i, ("stq", l, s)))
                            pe.wait_ge(k_stacked[s].sem, k_stacked[s].done(i, ("stk", l, s)))
                            if l < 2:
                                pe.wait_ge(mask_row[s].sem, mask_row[s].done(i, ("r0", l, s)))
                        n = max_full.order[step] - 1
                        pe.wait_ge(max_taken.sem, max_taken.ago(i, step, 2))
                        for k in range(2):
                            slot = 4 * hs + 2 * sp_ + k
                            if l == 1:
                                nc.tensor.matmul(max_ps[:, n % 2, k], ident_bf[:], bias_qk[:, t], start=True,
                                                 stop=False)
                            rows_ = slice(HROWS * h, HROWS * h + K_MAXPASS)
                            mm = nc.tensor.matmul(max_ps[:, n % 2, k], q_stack[rows_, s, slot, P * t:P * t + P],
                                                  k_stack[rows_, s, slot], start=(l != 1), stop=True)
                        mm.then_inc(max_full.sem, 1)
                    elif kind == "exp":
                        g, kt, h = step[3:]
                        if g % 2 == 0 and kt == 0 and h == 0:
                            pe.wait_ge(max_rows[g // 2].sem, max_rows[g // 2].done(i, ("nm", l, s, g // 2)))
                        n = exp_full.order[step] - 1
                        pe.wait_ge(probs_ready.sem, probs_ready.ago(i, step, 2))
                        for k in range(2):
                            slot = 2 * g + k
                            if l == 1:
                                nc.tensor.matmul(exp_ps[:, n % 2, k], ident_bf[:], bias_kq[:, kt], start=True,
                                                 stop=False)
                            rows_ = slice(HROWS * h, HROWS * h + K_EXPPASS)
                            mm = nc.tensor.matmul(exp_ps[:, n % 2, k], k_stack[rows_, s, slot, P * kt:P * kt + P],
                                                  q_stack[rows_, s, slot], start=(l != 1), stop=True)
                        mm.then_inc(exp_full.sem, 1)
                    elif kind == "pv":
                        g = step[3]
                        pe.wait_ge(probs_ready.sem, probs_ready.done(i, ("exp", l, s, g, TT - 1, HALVES - 1)))
                        if g == 0:
                            if l == 0:
                                pe.wait_ge(pool_v.sem, pool_v.done(i, ("v", 0, s)))
                            else:
                                ready(i, ("v", l, s))
                        n = pv_full.order[step] - 1
                        pe.wait_ge(normed.sem, normed.ago(i, step, 2))
                        for kt in range(TT):
                            for j in range(4):
                                h, k = j // 2, j % 2
                                head = SLOTS * h + 2 * g + k
                                mm = nc.tensor.matmul(pv_ps[32 * j:32 * j + 32, n % 2, 0:S],
                                                      v_ones[:, s, kt, head, :], probs[:, g % 2, 4 * h + 2 * kt + k],
                                                      start=(kt == 0), stop=(kt == TT - 1))
                        mm.then_inc(pv_full.sem, 1)


def kernel(**inputs):
    import numpy as _np
    import concourse.bacc as _bacc
    from concourse import mybir as _mybir
    from concourse.bass_utils import run_bass_kernel_spmd as _run

    a = {k: _np.asarray(v) for k, v in inputs.items()}
    f, s, d, g, j = 2, 8, 16, 4, 2
    nat = _np.arange(256)
    ds = nat.reshape(f, s, d).transpose(0, 2, 1).reshape(-1)
    comp = nat.reshape(f, g, j, d).transpose(0, 2, 3, 1).reshape(-1)
    L0, L1 = "L0_xattn_", "L1_xattn_"

    def tiles(v):
        return v.reshape(-1, 128).T

    ins = {
        "x": a["x"],
        "ctx_in": a["ctx_1024"][:, :, ds],
        "mask0": a["mask_Bx1x1xS2_if1"].reshape(16, 256),
        "mask1": a["mask_1x1xSxS_bk0"].reshape(256, 256).view(_np.int32),
        "wq_rep": _np.tile(a[L0 + "wq"].T, (1, s)),
        "wk_rep": _np.repeat(a[L0 + "wk"].T, s, axis=1),
        "wv_rep": _np.tile(_np.repeat(_np.repeat(a[L0 + "wv"].T, g, 0), g, 1), (j, j)),
        "w_out": a[L0 + "w_out"][comp],
        "wq1": a[L1 + "sa_wq"][:, ds], "wk1": a[L1 + "sa_wk"][:, ds], "wv1": a[L1 + "sa_wv"],
        "wq2": a[L1 + "ca_wq"][:, ds], "wk2": a[L1 + "ca_wk"][ds][:, ds], "wv2": a[L1 + "ca_wv"][ds],
        "wo1": a[L1 + "sa_wo"][comp], "wo2": a[L1 + "ca_wo"][comp],
        "wf1_0": a[L0 + "w_ff1"], "wf1_1": a[L1 + "ff_w1"],
        "wf2_0": a[L0 + "w_ff2"], "wf2_1": a[L1 + "ff_w2"],
        "rows": _np.stack([a[L0 + "g1"], a[L0 + "beta1"], a[L0 + "g2"], a[L0 + "beta2"],
                           a[L1 + "ln1_g"], a[L1 + "ln1_b"], a[L1 + "ln2_g"], a[L1 + "ln2_b"],
                           a[L1 + "ln3_g"], a[L1 + "ln3_b"],
                           a[L0 + "b_out"], a[L0 + "b_ff2"], a[L1 + "sa_bo"], a[L1 + "ca_bo"], a[L1 + "ff_b2"],
                           a[L1 + "sa_bv"], a[L1 + "ca_bv"]]).reshape(-1),
        "cols": _np.concatenate([tiles(a[L1 + "sa_bq"][ds]), tiles(a[L1 + "ca_bq"][ds]), tiles(a[L1 + "sa_bk"][ds]),
                                 tiles(a[L1 + "ca_bk"][ds]), tiles(a[L0 + "b_ff1"]), tiles(a[L1 + "ff_b1"])], 1),
    }
    slot_k, slot_m = nat[:128] // d, nat[:128] % s
    head = (nat[:128] // 64) * g + nat[:128] % g
    ins["ident"] = _np.eye(128, dtype=_np.float32)
    ins["same_slot"] = (slot_k[:, None] == slot_m[None, :]).astype(_np.float32)
    ins["same_head"] = (head[:, None] == head[None, :]).astype(_np.float32)

    nc = _bacc.Bacc("TRN2", target_bir_lowering=False, num_devices=1, dynamic_dma_scratch_size=1024)
    arrays, ap = {}, {}
    for name, v in ins.items():
        arrays[f"in_{name}"] = _np.ascontiguousarray(v)
        ap[name] = nc.dram_tensor(f"in_{name}", v.shape, _mybir.dt.from_np(v.dtype), kind="ExternalInput").ap()
    out = nc.dram_tensor("out_0", (16, 256, 256), _mybir.dt.float32, kind="ExternalOutput").ap()
    masks = nc.dram_tensor("masks_dram", (17, 256), _mybir.dt.float32, kind="Internal").ap()
    build(nc, ap["x"], ap["ctx_in"], ap["mask0"], ap["mask1"], ap["wq_rep"], ap["wk_rep"], ap["wv_rep"], ap["w_out"],
          [ap[n] for n in ("wq1", "wk1", "wv1", "wq2", "wk2", "wv2")], [ap["wo1"], ap["wo2"]],
          [ap["wf1_0"], ap["wf1_1"]], [ap["wf2_0"], ap["wf2_1"]], ap["rows"], ap["cols"], ap["ident"],
          ap["same_slot"], ap["same_head"], out, masks)
    r = _run(nc, [arrays], core_ids=[0])
    return r.results[0]["out_0"]
```

```python
from contextlib import ExitStack

import concourse.bass as bass
from concourse import mybir

ALU = mybir.AluOpType
ACT = mybir.ActivationFunctionType
AX = mybir.AxisListType
F32 = mybir.dt.float32
F32R = mybir.dt.float32r
BF16 = mybir.dt.bfloat16
I32 = mybir.dt.int32
U8 = mybir.dt.uint8

P = 128
B, S, E = 16, 256, 256
H, HD = 16, 16
FF = 1024
LANES = 2
NI = B // LANES
FT = E // P
TT = S // P
NF = FF // P
HALVES, SLOTS = 2, 8
GROUPS = 4
HROWS = 64
R_MASK, R_A, R_B, R_C, R_MAX = 0, 1, 17, 33, 49
K_MAXPASS, K_EXPPASS = 49, 51
EPS = 1e-5
L0_MASKED = -1e20 / 16.0
L1_MASKED = -1e30
ROWS = ["g0", "be0", "g1", "be1", "g2", "be2", "g3", "be3", "g4", "be4",
        "b_res0", "b_ff0", "b_o1", "b_o2", "b_ff1", "bv1", "bv2"]
RI = {n: i for i, n in enumerate(ROWS)}
C_Q, C_K, C_F = 0, 4, 8
NCOLS = 8 + 2 * NF
COSTS = {
    "load": [("sync", 0.9), ("wire", 3.5)], "r0": [("sync", 1.3), ("wire", 2.0)],
    "stq": [("sync", 3.8), ("wire", 2.0)], "stk": [("sync", 3.8), ("wire", 2.0)],
    "tc": [("tensor", 0.6), ("scalar", 0.6), ("vector", 0.7)], "tx": [("tensor", 0.6), ("scalar", 0.6)],
    "th": [("tensor", 0.6), ("scalar", 0.6), ("vector", 0.7)],
    "q": [("tensor", 2.0), ("scalar", 0.9), ("vector", 0.9)], "k": [("tensor", 2.0), ("scalar", 0.9), ("vector", 0.9)],
    "v": [("tensor", 2.0), ("vector", 0.8)], "v_copy": [("gpsimd", 3.6)],
    "max": [("tensor", 0.4), ("vector", 0.65)],
    "nm": [("vector", 0.6), ("tensor", 0.2), ("scalar", 0.4), ("sync", 1.3), ("wire", 2.0)],
    "exp": [("tensor", 0.4), ("scalar", 0.55)], "pv": [("tensor", 1.4), ("vector", 1.2)],
    "oc": [("vector", 0.7), ("sync", 2.5), ("wire", 2.0)], "o": [("tensor", 2.2), ("vector", 0.7)],
    "ls": [("vector", 1.1), ("gpsimd", 1.0)], "ln": [("vector", 1.8), ("gpsimd", 1.5)],
    "ff1": [("tensor", 1.8), ("scalar", 0.9)], "ff2": [("tensor", 8.0), ("vector", 0.7)],
    "store": [("sync", 0.5), ("wire", 3.0)]}
HELD = [(("max",), ("oc",)), (("tx", "ff1"), ("q", "ff2")), (("q",), ("stq",)), (("k",), ("stk",)), (("load",), ("v",))]

SETUP_LOADS, SETUP_DMAS = 15, 25
SETUP_ACT = 2
SETUP_DVE_CHAIN = 17
SETUP_DVE = SETUP_DVE_CHAIN + 1


def needed(x):
    kind, l, s = x[:3]
    if kind in ("tc", "tx"):
        return [("load", 0, s)]
    if kind == "th":
        return [("ln", (0, 2, 3, 4)[l], s)]
    if kind == "q":
        return [("th", l, s) if l else ("tx", 0, s)]
    if kind in ("k", "v"):
        return [("th", 1, s)] if l == 1 else [("tc", 0, s)]
    if kind == "stq":
        return [("q", l, s)]
    if kind == "stk":
        return [("k", l, s) if l else ("tc", 0, s)]
    if kind == "max":
        return [("stq", l, s), ("stk", l, s)] + ([("r0", l, s)] if l < 2 else [])
    if kind == "nm":
        return [("max", l, s, x[3], TT - 1, 1, HALVES - 1)]
    if kind == "exp":
        return [("nm", l, s, x[3] // 2)]
    if kind == "pv":
        return [("exp", l, s, x[3], TT - 1, HALVES - 1), ("v", l, s)]
    if kind == "oc":
        return [("pv", l, s, GROUPS - 1)]
    if kind == "o":
        return [("oc", l, s)]
    if kind == "ls":
        return [(("o", 0, s), ("ff2", 0, s), ("ln", 1, s), ("o", 1, s), ("o", 2, s))[l]]
    if kind == "ln":
        return [("ls", l, s)]
    if kind == "ff1":
        return [("th", 3 * l, s)]
    if kind == "ff2":
        return [("ff1", l, s, NF // 2 - 1)]
    return [("ff2", 1, s)] if kind == "store" else []


def merge(a, b):
    clock, done, ring, owner = {}, {}, {}, {}
    lanes, out = [list(a), list(b)], []

    def cost(x):
        return COSTS["v_copy" if x[:2] == ("v", 0) else x[0]]

    def held(x):
        return [n for n, (first, last) in enumerate(HELD) if x[0] in first]

    def start(x):
        if any(owner.get(n, x[2]) != x[2] for n in held(x)):
            return None
        kind = "dense" if is_dense(x) else x[0]
        waits = [done.get(y, 0.0) for y in needed(x)] + [clock.get(cost(x)[0][0], 0.0)]
        if kind in ("dense", "max", "exp", "pv"):
            waits.append(ring.get(kind, (0.0, 0.0))[0])
        return max(waits)

    def take(x):
        now = start(x)
        for n in held(x):
            owner[n] = x[2]
        for n, (first, last) in enumerate(HELD):
            if x[0] in last and owner.get(n) == x[2]:
                del owner[n]
        for engine, us in cost(x):
            now = max(now + 0.1, clock.get(engine, 0.0) if engine != "wire" else 0.0) + us
            clock[engine] = now
        done[x] = now
        kind = "dense" if is_dense(x) else x[0]
        ring[kind] = (ring.get(kind, (0.0, 0.0))[1], now)
        out.append(x)

    def left(steps):
        return sum(us for x in steps for engine, us in cost(x))

    while any(lanes):
        ready = [(start(lane[0]), -left(lane), n) for n, lane in enumerate(lanes) if lane and start(lane[0]) is not None]
        take(lanes[min(ready)[2]].pop(0))
    return out


def enter(s):
    return [("load", 0, s), ("tc", 0, s), ("tx", 0, s), ("q", 0, s), ("r0", 0, s), ("stk", 0, s), ("stq", 0, s),
            ("v", 0, s)]


def attend(l, s):
    def maxes(hs):
        return [("max", l, s, hs, t, sp, h) for t in range(TT) for sp in range(2) for h in range(HALVES)]

    def group(g):
        return [("exp", l, s, g, kt, h) for kt in range(TT) for h in range(HALVES)] + [("pv", l, s, g)]
    second = maxes(1)
    beside = group(0) + group(1)[:2]
    mixed = [x for pair in zip(beside, second[4:] + [None] * len(beside)) for x in pair if x]
    return (maxes(0) + [("nm", l, s, 0)] + second[:4] + mixed + [("nm", l, s, 1)] + group(1)[2:] + group(2)
            + group(3) + [("oc", l, s)])


def ffn(f, s):
    return [("ff1", f, s, c) for c in range(NF // 2)] + [("ff2", f, s)]


def after0(s):
    return [("o", 0, s), ("ls", 0, s), ("ln", 0, s), ("th", 0, s)] + ffn(0, s)


def before1(s):
    return [("ls", 1, s), ("ln", 1, s), ("ls", 2, s), ("ln", 2, s), ("th", 1, s), ("r0", 1, s), ("k", 1, s), ("stk", 1, s), ("q", 1, s),
            ("stq", 1, s), ("v", 1, s)]


def between(s):
    return [("k", 2, s), ("stk", 2, s), ("v", 2, s), ("o", 1, s), ("ls", 3, s), ("ln", 3, s), ("th", 2, s), ("q", 2, s),
            ("stq", 2, s)]


def leave(s):
    return [("o", 2, s), ("ls", 4, s), ("ln", 4, s), ("th", 3, s)] + ffn(1, s) + [("store", 0, s)]


def second_half(s):
    return attend(1, s) + between(s) + attend(2, s) + leave(s)


def first_half(s):
    return enter(s) + attend(0, s) + after0(s) + before1(s)


DENSE = ("tx", "tc", "q", "k", "nm", "o", "th", "ff1", "ff2")


def is_dense(x):
    return x[0] in DENSE or (x[0] == "v" and x[1] > 0)


LOOP = merge(second_half(0), first_half(1)) + merge(second_half(1), first_half(0))
OPENING = first_half(0)
CLOSING = merge(second_half(0), first_half(1)) + second_half(1)
PEELED = OPENING + CLOSING
N_LOOP = NI - 1


class Run:

    def __init__(self, steps, i=None):
        self.steps, self.i, self.looped = steps, i, int(i is not None)
        self.at = {x: n for n, x in enumerate(LOOP if self.looped else PEELED)}

    def sequence_number(self, step):
        ahead = step[0] != "store" and step[2] == 0
        if self.looped:
            return self.i * LANES + (LANES if ahead else step[2])
        return 0 if ahead else B - LANES + step[2]


class Signal:

    def __init__(self, peeled, in_loop, steps, inc):
        self.sems, self.inc, self.steps = (peeled, in_loop), inc, steps
        self.order = tuple({x: n + 1 for n, x in enumerate(seq)} for seq in steps)
        self.per = inc * len(steps[1])

    def number(self, run, x):
        return self.order[run.looped][x] - 1

    def sem(self, run):
        return self.sems[run.looped]

    def await_count(self, eng, run, count):
        if run.looped:
            eng.wait_ge(self.sems[1], run.i * self.per + (self.per + count))
        elif count > 0:
            eng.wait_ge(self.sems[0], count)

    def wait(self, eng, run, step, x=None, part=0):
        x = x or step
        count = self.order[run.looped][x] * self.inc - (self.inc - part if part else 0)
        if run.at[x] > run.at[step]:
            count -= self.per if run.looped else count
        self.await_count(eng, run, count)

    def wait_last(self, eng, run, step, chosen=lambda x: True):
        found = [x for x in self.steps[run.looped] if chosen(x)]
        ahead = [x for x in found if run.at[x] < run.at[step]]
        if ahead:
            self.await_count(eng, run, self.order[run.looped][ahead[-1]] * self.inc)
        elif run.looped:
            self.await_count(eng, run, self.order[1][found[-1]] * self.inc - self.per)

    def wait_ago(self, eng, run, x, back=1):
        self.await_count(eng, run, (self.order[run.looped][x] - back) * self.inc)

    def total(self, run):
        if run.looped:
            return self.per * (N_LOOP + 1)
        return self.inc * sum(x in self.order[0] for x in PEELED[:run.at[run.steps[-1]] + 1])


def build(nc, x, ctx_in, mask0, mask1, wq_rep, wk_rep, wv_rep, w_out, wqkv, wo, wff1, wff2, rows, cols, ident_in,
          same_slot, same_head, out, masks_dram):
    every = []

    with ExitStack() as ctx:
        def sb(name, shape, dt=F32):
            return ctx.enter_context(nc.sbuf_tensor(name, shape, dt))

        def sem(name):
            return ctx.enter_context(nc.semaphore(name))

        def signal(name, inc, *chosen):
            picked = chosen if len(chosen) == 2 else [[x for x in seq if chosen[0](x)] for seq in (PEELED, LOOP)]
            every.append(Signal(sem(name + "_once"), sem(name), tuple(picked), inc))
            return every[-1]

        def each_lane(name, inc, chosen):
            return [signal(f"{name}{s}", inc, lambda x, s=s: x[2] == s and chosen(x)) for s in range(LANES)]

        def kinds(*names):
            return lambda x: x[0] in names

        dense_ps = ctx.enter_context(nc.psum_tensor("dense_ps", [P, 2, 2, 256], F32))
        max_ps = ctx.enter_context(nc.psum_tensor("max_ps", [P, 2, 2, 256], F32))
        exp_ps = ctx.enter_context(nc.psum_tensor("exp_ps", [P, 2, 2, 256], F32))
        pv_ps = ctx.enter_context(nc.psum_tensor("pv_ps", [P, 2, 512], F32))

        qkv_w = sb("qkv_w", [P, 6, 2, FT, E], F32R)
        ff1_w = sb("ff1_w", [P, 2, 2, FT, FF], F32R)
        ff2_w = sb("ff2_w", [P, 2, NF, E])
        o_w = sb("o_w", [P, 3, FT, E])
        q0_w = sb("q0_w", [P, P])
        row = sb("row", [P, len(ROWS), E])
        col = sb("col", [P, NCOLS])
        ident = sb("ident", [P, P])
        ident_bf = sb("ident_bf", [P, P], BF16)
        bias_qk = sb("bias_qk", [P, TT, S], BF16)
        bias_kq = sb("bias_kq", [P, TT, S], BF16)
        nan_col = sb("nan_col", [P, TT])
        minus_half = sb("minus_half", [P, TT])

        x_tok = sb("x_tok", [P, TT, E])
        ctx_tok = sb("ctx_tok", [P, TT, E])
        ctxT = sb("ctxT", [P, LANES, 2, FT, S], F32R)
        qT = sb("qT", [P, 2, FT, S], F32R)
        kT = sb("kT", [P, 2, FT, S], F32R)
        q_stack = sb("q_stack", [P, LANES, SLOTS, S], F32R)
        k_stack = sb("k_stack", [P, LANES, SLOTS, S], F32R)
        v_ones = sb("v_ones", [P, LANES, TT, H, 2 * HD])
        m_tok = sb("m_tok", [P, 2, TT, 8])
        nm_tok = sb("nm_tok", [P, 2, TT, P])
        nmT = sb("nmT", [16, 2, S], F32R)
        probs = sb("probs", [P, 2, HALVES * TT * 2, S])
        pv_t = sb("pv_t", [P, 2, S])
        inverse = sb("inverse", [P, 2, S // 32, 1])
        attn_pad = sb("attn_pad", [P, GROUPS, S])
        attn = sb("attn", [P, FT, S])
        res = sb("res", [P, LANES, TT, E])
        y = sb("y", [P, LANES, TT, E])
        z = sb("z", [P, TT, E])
        hx = sb("hx", [P, LANES, TT, E])
        hT = sb("hT", [P, LANES, 2, FT, S], F32R)
        hid = sb("hid", [P, NF, S])
        xT = hid[:, 0:FT, :]
        st = sb("st", [P, LANES, TT, 6])
        mv = sb("mv", [P, LANES, TT, 2])
        rstd = sb("rstd", [P, LANES, TT])
        vare = sb("vare", [P, LANES, TT])

        loaded = each_lane("loaded", 32, kinds("load"))
        dense_full = signal("dense_full", 1, is_dense)
        evacuated = [signal(f"evacuated{b}", 2, dense_full.steps[0][b::2], dense_full.steps[1][b::2])
                     for b in range(2)]
        pool_v = signal("pool_v", 1, lambda x: x[:2] == ("v", 0))
        q_stacked = each_lane("q_stacked", 96, kinds("stq"))
        k_stacked = each_lane("k_stacked", 96, kinds("stk"))
        mask_row = each_lane("mask_row", 32, kinds("r0"))
        max_full = signal("max_full", 1, kinds("max"))
        max_taken = signal("max_taken", 1, kinds("max"))
        neg_hi = signal("neg_hi", 2, kinds("nm"))
        neg_lo = signal("neg_lo", 1, kinds("nm"))
        max_rows = [signal(f"max_rows{hs}", 32, lambda x, hs=hs: x[0] == "nm" and x[3] == hs) for hs in range(2)]
        exp_full = signal("exp_full", 1, kinds("exp"))
        probs_ready = signal("probs_ready", 1, kinds("exp"))
        pv_full = signal("pv_full", 1, kinds("pv"))
        pv_turned = signal("pv_turned", 1, kinds("pv"))
        inverted = signal("inverted", 1, kinds("pv"))
        normed = signal("normed", 1, kinds("pv"))
        turned_back = signal("turned_back", 1, kinds("pv"))
        compacted = signal("compacted", 64, kinds("oc"))
        stats_part = signal("stats_part", 1, kinds("ls"))
        stats = signal("stats", 1, kinds("ls"))
        eps_added = signal("eps_added", 1, kinds("ls"))
        rstd_ready = signal("rstd_ready", 1, kinds("ls"))
        scaled = signal("scaled", 1, kinds("ln"))
        ln_done = signal("ln_done", 1, kinds("ln"))
        res_ready = signal("res_ready", 1, lambda x: x[:2] == ("v", 0) or x[0] == "ln" and x[1] != 2)
        stored = each_lane("stored", 16, kinds("store"))
        by_dma = [*loaded, *q_stacked, *k_stacked, *mask_row, *max_rows, compacted, *stored]
        assert all(len(sg.steps[1]) % 2 == 0 for sg in (dense_full, max_full, exp_full, pv_full))

        def bank(run, x):
            return dense_full.number(run, x) % 2

        def evac(run, x):
            return evacuated[bank(run, x)]

        def product(run, x):
            return dense_ps[:, bank(run, x)]

        primed = sem("primed")
        s_const = sem("s_const")
        s_raw = [sem("s_raw0"), sem("s_raw1")]
        s_hi = sem("s_hi")
        s_lo = sem("s_lo")
        s_dve = sem("s_dve")
        s_pe = sem("s_pe")
        s_act = sem("s_act")
        carrier = sem("carrier")
        carrier_sp = sem("carrier_sp")
        carrier_dve = sem("carrier_dve")

        stage = probs[:].rearrange("p a b e -> p a (b e)")

        splits = []
        for n in range(6):
            splits.append((qkv_w[:, n, 0].rearrange("p k e -> p (k e)"), qkv_w[:, n, 1].rearrange("p k e -> p (k e)"),
                           wqkv[n], FT, 0.25 if n % 3 == 0 else 1.0))
        for f in range(2):
            splits.append((ff1_w[:, f, 0].rearrange("p k e -> p (k e)"), ff1_w[:, f, 1].rearrange("p k e -> p (k e)"),
                           wff1[f], FT, 1.0))

        def sync_steps(sp, run):
            def hold():
                sp.sem_inc(carrier_sp, 1)

            for step in run.steps:
                kind, l, s = step[:3]
                if kind == "load":
                    dense_full.wait_last(sp, run, step, kinds("tx"))
                    hold()
                    res_ready.wait_last(sp, run, step, kinds("v"))
                    hold()
                    b = run.sequence_number(step)
                    sp.dma_start(ctx_tok[:], ctx_in[bass.ds(b, 1)].rearrange("a (t p) e -> p (a t) e", p=P)
                                 ).then_inc(loaded[s].sem(run), 16)
                    sp.dma_start(x_tok[:], x[bass.ds(b, 1)].rearrange("a (t p) e -> p (a t) e", p=P)
                                 ).then_inc(loaded[s].sem(run), 16)
                elif kind == "r0":
                    exp_full.wait_last(sp, run, step, lambda x: x[2] == s)
                    hold()
                    src = masks_dram[bass.ds(run.sequence_number(step), 1)] if l == 0 else masks_dram[B:B + 1]
                    for h in range(HALVES):
                        sp.dma_start(k_stack[HROWS * h:HROWS * h + 1, s].bitcast(F32),
                                     src.rearrange("a (o k) -> a o k", o=1).to_broadcast([1, SLOTS, S])
                                     ).then_inc(mask_row[s].sem(run), 16)
                elif kind in ("stq", "stk"):
                    key = ("q" if kind == "stq" else "k", l, s)
                    if kind == "stk" and l == 0:
                        key = ("tc", 0, s)
                    evac(run, key).wait(sp, run, step, key)
                    hold()
                    exp_full.wait_last(sp, run, step, lambda x: x[2] == s)
                    hold()
                    sg = (q_stacked if kind == "stq" else k_stacked)[s]
                    dst, parts = (q_stack, (0, 0, 1)) if kind == "stq" else (k_stack, (0, 1, 0))
                    for r, part in zip((R_A, R_B, R_C), parts):
                        for h in range(HALVES):
                            src = (qT if kind == "stq" else kT)[:, part, h, :]
                            if kind == "stk" and l == 0:
                                src = ctxT[:, s, part, h, :]
                            sp.dma_start(dst[HROWS * h + r:HROWS * h + r + HD, s].bitcast(F32), src.bitcast(F32)
                                         ).then_inc(sg.sem(run), 16)
                elif kind == "nm":
                    hs = step[3]
                    evac(run, step).wait(sp, run, step)
                    hold()
                    exp_full.wait_last(sp, run, step, lambda x: x[2] == s and x[3] // 2 == hs)
                    hold()
                    for h in range(HALVES):
                        sp.dma_start(q_stack[HROWS * h + R_MAX:HROWS * h + R_MAX + 2, s, 4 * hs:4 * hs + 4
                                             ].bitcast(F32),
                                     nmT[8 * h:8 * h + 8, hs, :].bitcast(F32)).then_inc(max_rows[hs].sem(run), 16)
                elif kind == "oc":
                    turned_back.wait(sp, run, step, ("pv", l, s, GROUPS - 1))
                    hold()
                    dense_full.wait_last(sp, run, step, kinds("o"))
                    hold()
                    for j in range(4):
                        sp.dma_start(attn[64 * (j % 2):64 * (j % 2) + 64, j // 2, :],
                                     attn_pad[32 * j:32 * j + HD]).then_inc(compacted.sem(run), 16)
                elif kind == "store":
                    evac(run, ("ff2", 1, s)).wait(sp, run, step, ("ff2", 1, s))
                    hold()
                    b = run.sequence_number(step)
                    sp.dma_start(out[bass.ds(b, 1)].rearrange("a (t p) e -> p (a t) e", p=P), y[:, s]
                                 ).then_inc(stored[s].sem(run), 16)

        def finish_dmas(sp, run):
            for sg in by_dma:
                sp.wait_ge(sg.sem(run), sg.total(run))

        def pool_steps(pool, run):
            def hold():
                pool.sem_inc(carrier, 1)

            for step in run.steps:
                kind, l, s = step[:3]
                if kind == "v" and l == 0:
                    loaded[s].wait(pool, run, step, ("load", 0, s))
                    hold()
                    pv_full.wait_last(pool, run, step, lambda x: x[2] == s)
                    hold()
                    for t in range(TT):
                        for h in range(HALVES):
                            last = nc.gpsimd.tensor_copy(
                                v_ones[:, s, t, SLOTS * h:SLOTS * h + SLOTS, 0:HD],
                                ctx_tok[:, t, P * h:P * h + P].rearrange("p (d s) -> p s d", d=HD))
                    last.then_inc(pool_v.sem(run), 1)
                    evac(run, ("ff2", 1, s)).wait(pool, run, step, ("ff2", 1, s))
                    hold()
                    for t in range(TT):
                        last = nc.gpsimd.tensor_tensor(res[:, s, t], x_tok[:, t], row[:, RI["b_res0"]], ALU.add)
                    last.then_inc(res_ready.sem(run), 1)
                elif kind == "ls":
                    stats.wait(pool, run, step)
                    hold()
                    nc.gpsimd.tensor_scalar(vare[:, s], mv[:, s, :, 1], EPS, None, ALU.add
                                            ).then_inc(eps_added.sem(run), 1)
                    eps_added.wait(pool, run, step)
                    nc.gpsimd.tensor_tensor(rstd[:, s], vare[:, s], minus_half[:], ALU.pow
                                            ).then_inc(rstd_ready.sem(run), 1)
                elif kind == "ln" and l != 2:
                    if l < 2:
                        ln_done.wait(pool, run, step)
                    hold()
                    src = hx if l == 0 else y
                    b = {0: "b_ff0", 1: "b_o1", 3: "b_o2", 4: "b_ff1"}[l]
                    for t in range(TT):
                        last = nc.gpsimd.tensor_tensor(res[:, s, t], src[:, s, t], row[:, RI[b]], ALU.add)
                    last.then_inc(res_ready.sem(run), 1)

        def scalar_steps(act, run):
            for step in run.steps:
                kind, l, s = step[:3]
                if is_dense(step) and kind not in ("v", "o", "ff2"):
                    d = product(run, step)
                    ev = evac(run, step).sem(run)
                    dense_full.wait(act, run, step)
                if kind == "tc":
                    k_stacked[s].wait_last(act, run, step)
                    nc.scalar.activation(ctxT[:, s, 0], d, ACT.Copy).then_inc(ev, 1)
                elif kind == "tx":
                    nc.scalar.activation(xT, d, ACT.Copy).then_inc(ev, 2)
                elif kind in ("q", "k"):
                    for sg in q_stacked if kind == "q" else k_stacked:
                        sg.wait_last(act, run, step, lambda x: kind == "q" or x[1] > 0)
                    dst = (qT if kind == "q" else kT)
                    if l == 0:
                        nc.scalar.activation(dst[:, 0], d, ACT.Copy).then_inc(ev, 1)
                    else:
                        c = (C_Q if kind == "q" else C_K) + (l - 1) * FT
                        for f in range(FT):
                            last = nc.scalar.activation(dst[:, 0, f], d[:, f], ACT.Identity,
                                                        bias=col[:, c + f:c + f + 1])
                        last.then_inc(ev, 1)
                elif kind == "nm":
                    max_rows[step[3]].wait_ago(act, run, step)
                    nc.scalar.activation(nmT[:, step[3]], d.rearrange("p a q -> p (a q)")[0:16, 0:S], ACT.Copy
                                         ).then_inc(ev, 2)
                elif kind == "th":
                    nc.scalar.activation(hT[:, s, 0], d, ACT.Copy).then_inc(ev, 1)
                elif kind == "ff1":
                    for f in range(2):
                        m = 2 * step[3] + f
                        c = C_F + l * NF + m
                        last = nc.scalar.activation(hid[:, m], d[:, f], ACT.Relu, bias=col[:, c:c + 1])
                    last.then_inc(ev, 2)
                elif kind == "exp":
                    g, kt, h = step[3:]
                    exp_full.wait(act, run, step)
                    if kt == 0 and h == 0:
                        pv_full.wait_ago(act, run, ("pv", l, s, g), 2)
                    nc.scalar.activation(probs[:, g % 2, 4 * h + 2 * kt:4 * h + 2 * kt + 2],
                                         exp_ps[:, exp_full.number(run, step) % 2], ACT.Exp
                                         ).then_inc(probs_ready.sem(run), 1)

        def vector_steps(dve, run):
            def hold():
                dve.sem_inc(carrier_dve, 1)

            def normalise(x):
                n = pv_full.number(run, x) % 2
                inverted.wait(dve, run, step, x)
                blocks = pv_t[:, n].rearrange("p (b r) -> p b r", r=32)
                nc.vector.tensor_tensor(blocks[:, :, 0:HD], blocks[:, :, 0:HD],
                                        inverse[:, n].to_broadcast([P, S // 32, HD]), ALU.mult
                                        ).then_inc(normed.sem(run), 1)

            def turn_back(x):
                if x[3] == 0:
                    compacted.wait_last(dve, run, step)
                    hold()
                normed.wait(dve, run, step, x)
                nc.vector.transpose(attn_pad[:, x[3]], pv_t[:, pv_full.number(run, x) % 2]
                                    ).then_inc(turned_back.sem(run), 1)

            for step in run.steps:
                kind, l, s = step[:3]
                if is_dense(step):
                    d = product(run, step)
                    ev = evac(run, step)
                if kind == "tc":
                    ev.wait(dve, run, step, part=1)
                    nc.vector.tensor_tensor(ctxT[:, s, 1], d, ctxT[:, s, 0].bitcast(F32), ALU.subtract
                                            ).then_inc(ev.sem(run), 1)
                elif kind in ("q", "k"):
                    ev.wait(dve, run, step, part=1)
                    dst = qT if kind == "q" else kT
                    if l == 0:
                        nc.vector.tensor_tensor(dst[:, 1], d, dst[:, 0].bitcast(F32), ALU.subtract
                                                ).then_inc(ev.sem(run), 1)
                    else:
                        c = (C_Q if kind == "q" else C_K) + (l - 1) * FT
                        for f in range(FT):
                            last = nc.vector.scalar_tensor_tensor(dst[:, 1, f], d[:, f], col[:, c + f:c + f + 1],
                                                                  dst[:, 0, f].bitcast(F32), ALU.add, ALU.subtract)
                        last.then_inc(ev.sem(run), 1)
                elif kind == "th":
                    ev.wait(dve, run, step, part=1)
                    nc.vector.tensor_tensor(hT[:, s, 1], d, hT[:, s, 0].bitcast(F32), ALU.subtract
                                            ).then_inc(ev.sem(run), 1)
                elif kind == "v" and l > 0:
                    dense_full.wait(dve, run, step)
                    for t in range(TT):
                        last = nc.vector.tensor_tensor(
                            v_ones[:, s, t, :, 0:HD], d[:, t].rearrange("p (h e) -> p h e", h=H),
                            row[:, RI[f"bv{l}"]].rearrange("p (h e) -> p h e", h=H), ALU.add)
                    last.then_inc(ev.sem(run), 2)
                elif kind == "max":
                    hs, t, sp_, h = step[3:]
                    max_full.wait(dve, run, step)
                    if t == 0 and sp_ == 0 and h == 0:
                        neg_lo.wait_last(dve, run, step, lambda x: x[3] == hs)
                    c = 4 * h + 2 * sp_
                    nc.vector.tensor_reduce(m_tok[:, hs, t, c:c + 2], max_ps[:, max_full.number(run, step) % 2],
                                            AX.X, ALU.max).then_inc(max_taken.sem(run), 1)
                elif kind == "nm":
                    hs = step[3]
                    max_taken.wait(dve, run, step, ("max", l, s, hs, TT - 1, 1, HALVES - 1))
                    dense_full.wait_last(dve, run, step, lambda x: x[0] == "nm" and x[3] == hs)
                    for t in range(TT):
                        v4 = nm_tok[:, hs, t, 0:16].rearrange("p (h c k) -> p c h k", h=2, c=2)
                        m4 = m_tok[:, hs, t].rearrange("p (h k) -> p h k", h=2)
                        hi = v4[:, 0].bitcast(F32R)
                        if l == 1:
                            ins = nc.vector.tensor_scalar(hi, m4, -1.0, nan_col[:, t:t + 1], ALU.mult, ALU.add)
                        else:
                            ins = nc.vector.tensor_scalar(hi, m4, -1.0, None, ALU.mult)
                        ins.then_inc(neg_hi.sem(run), 1)
                    neg_hi.wait(dve, run, step)
                    for t in range(TT):
                        v4 = nm_tok[:, hs, t, 0:16].rearrange("p (h c k) -> p c h k", h=2, c=2)
                        m4 = m_tok[:, hs, t].rearrange("p (h k) -> p h k", h=2)
                        last = nc.vector.scalar_tensor_tensor(v4[:, 1], m4, -1.0, v4[:, 0], ALU.mult, ALU.subtract)
                    last.then_inc(neg_lo.sem(run), 1)
                elif kind == "pv":
                    n = pv_full.number(run, step) % 2
                    before = ("pv", l, s, step[3] - 1) if step[3] else None
                    pv_full.wait(dve, run, step)
                    hold()
                    turned_back.wait_ago(dve, run, step, 2)
                    nc.vector.transpose(pv_t[:, n], pv_ps[:, n, 0:S]).then_inc(pv_turned.sem(run), 1)
                    if before:
                        normalise(before)
                    pv_turned.wait(dve, run, step)
                    nc.vector.reciprocal(inverse[:, n], pv_t[:, n].rearrange("p (b r) -> p b r", r=32)[:, :, HD:HD + 1]
                                         ).then_inc(inverted.sem(run), 1)
                    if before:
                        turn_back(before)
                elif kind == "oc":
                    normalise(("pv", l, s, GROUPS - 1))
                    turn_back(("pv", l, s, GROUPS - 1))
                elif kind == "o" or kind == "ff2":
                    dense_full.wait(dve, run, step)
                    res_ready.wait(dve, run, step, {("o", 0): ("v", 0, s), ("ff2", 0): ("ln", 0, s),
                                                    ("o", 1): ("ln", 1, s), ("o", 2): ("ln", 3, s),
                                                    ("ff2", 1): ("ln", 4, s)}[kind, l])
                    if kind == "o":
                        stored[s].wait_last(dve, run, step)
                    nc.vector.tensor_tensor(y[:, s], d, res[:, s], ALU.add).then_inc(ev.sem(run), 2)
                elif kind == "ls":
                    src = {0: ("o", 0, s), 1: ("ff2", 0, s), 2: ("ln", 1, s), 3: ("o", 1, s), 4: ("o", 2, s)}[l]
                    if l == 2:
                        ln_done.wait(dve, run, step, src)
                    else:
                        evac(run, src).wait(dve, run, step, src)
                    for t in range(TT):
                        last = nc.vector.bn_stats(st[:, s, t], y[:, s, t])
                    last.then_inc(stats_part.sem(run), 1)
                    eps_added.wait_last(dve, run, step, lambda x: x[2] == s)
                    hold()
                    stats_part.wait(dve, run, step)
                    hold()
                    for t in range(TT):
                        last = nc.vector.bn_aggr(mv[:, s, t], st[:, s, t])
                    last.then_inc(stats.sem(run), 1)
                elif kind == "ln":
                    stats.wait(dve, run, step, ("ls", l, s))
                    for t in range(TT):
                        last = nc.vector.scalar_tensor_tensor(z[:, t], y[:, s, t], mv[:, s, t, 0:1],
                                                              row[:, RI[f"g{l}"]], ALU.subtract, ALU.mult)
                    last.then_inc(scaled.sem(run), 1)
                    scaled.wait(dve, run, step)
                    rstd_ready.wait(dve, run, step, ("ls", l, s))
                    dst = y if l == 1 else hx
                    for t in range(TT):
                        last = nc.vector.scalar_tensor_tensor(dst[:, s, t], z[:, t], rstd[:, s, t:t + 1],
                                                              row[:, RI[f"be{l}"]], ALU.mult, ALU.add)
                    last.then_inc(ln_done.sem(run), 1)

        def tensor_steps(pe, run):
            def split_product(ps, w, mov):
                for n, (a, b) in enumerate([(0, 0), (1, 0), (0, 1)]):
                    for k in range(FT):
                        mm = nc.tensor.matmul(ps, w(a, k), mov(b, k), start=(n == 0 and k == 0),
                                              stop=(n == 2 and k == FT - 1))
                return mm

            for step in run.steps:
                kind, l, s = step[:3]

                def ready(key):
                    if not (is_dense(step) and bank(run, key) == bank(run, step)):
                        evac(run, key).wait(pe, run, step, key)

                if is_dense(step):
                    d = product(run, step)
                    evac(run, step).wait_ago(pe, run, step)
                if kind in ("tc", "tx", "th"):
                    if kind == "th":
                        ln_done.wait(pe, run, step, ("ln", {0: 0, 1: 2, 2: 3, 3: 4}[l], s))
                        src = hx[:, s]
                    else:
                        loaded[s].wait(pe, run, step, ("load", 0, s))
                        src = ctx_tok if kind == "tc" else x_tok
                    for f in range(FT):
                        for t in range(TT):
                            mm = nc.tensor.transpose(d[:, f, P * t:P * t + P], src[:, t, P * f:P * f + P], ident[:])
                    mm.then_inc(dense_full.sem(run), 1)
                elif kind == "q" and l == 0:
                    ready(("tx", 0, s))
                    for f in range(FT):
                        mm = nc.tensor.matmul(d[:, f], q0_w[:], xT[:, f], start=True, stop=True)
                    mm.then_inc(dense_full.sem(run), 1)
                elif kind in ("q", "k"):
                    w = 3 * (l - 1) + (kind == "k")
                    own = kind == "q" or l == 1
                    ready(("th", l, s) if own else ("tc", 0, s))
                    src = hT[:, s] if own else ctxT[:, s]
                    for f in range(FT):
                        mm = split_product(d[:, f], lambda a, k: qkv_w[:, w, a, k, P * f:P * f + P],
                                           lambda b, k: src[:, b, k])
                    mm.then_inc(dense_full.sem(run), 1)
                elif kind == "v" and l > 0:
                    w = 3 * (l - 1) + 2
                    src = hT[:, s] if l == 1 else ctxT[:, s]
                    for t in range(TT):
                        mm = split_product(d[:, t], lambda a, k: src[:, a, k, P * t:P * t + P],
                                           lambda b, k: qkv_w[:, w, b, k])
                    mm.then_inc(dense_full.sem(run), 1)
                elif kind == "nm":
                    neg_lo.wait(pe, run, step)
                    dd = d.rearrange("p a q -> p (a q)")
                    for t in range(TT):
                        mm = nc.tensor.transpose(dd[:, P * t:P * t + P], nm_tok[:, step[3], t], ident[:])
                    mm.then_inc(dense_full.sem(run), 1)
                elif kind == "o":
                    compacted.wait(pe, run, step, ("oc", l, s))
                    for t in range(TT):
                        for k in range(FT):
                            mm = nc.tensor.matmul(d[:, t], attn[:, k, P * t:P * t + P], o_w[:, l, k],
                                                  start=(k == 0), stop=(k == FT - 1))
                    mm.then_inc(dense_full.sem(run), 1)
                elif kind == "ff1":
                    if step[3] == 0:
                        ready(("th", 0 if l == 0 else 3, s))
                    for f in range(2):
                        m = 2 * step[3] + f
                        mm = split_product(d[:, f], lambda a, k: ff1_w[:, l, a, k, P * m:P * m + P],
                                           lambda b, k: hT[:, s, b, k])
                    mm.then_inc(dense_full.sem(run), 1)
                elif kind == "ff2":
                    last_two = [("ff1", l, s, c) for c in range(NF // 2 - 2, NF // 2)]
                    if bank(run, last_two[0]) != bank(run, last_two[1]):
                        ready(last_two[0])
                    ready(last_two[1])
                    for t in range(TT):
                        for k in range(NF):
                            mm = nc.tensor.matmul(d[:, t], hid[:, k, P * t:P * t + P], ff2_w[:, l, k],
                                                  start=(k == 0), stop=(k == NF - 1))
                    mm.then_inc(dense_full.sem(run), 1)
                elif kind == "max":
                    hs, t, sp_, h = step[3:]
                    if hs == 0 and t == 0 and sp_ == 0 and h == 0:
                        q_stacked[s].wait(pe, run, step, ("stq", l, s))
                        k_stacked[s].wait(pe, run, step, ("stk", l, s))
                        if l < 2:
                            mask_row[s].wait(pe, run, step, ("r0", l, s))
                    n = max_full.number(run, step) % 2
                    max_taken.wait_ago(pe, run, step, 2)
                    for k in range(2):
                        slot = 4 * hs + 2 * sp_ + k
                        if l == 1:
                            nc.tensor.matmul(max_ps[:, n, k], ident_bf[:], bias_qk[:, t], start=True, stop=False)
                        rows_ = slice(HROWS * h, HROWS * h + K_MAXPASS)
                        mm = nc.tensor.matmul(max_ps[:, n, k], q_stack[rows_, s, slot, P * t:P * t + P],
                                              k_stack[rows_, s, slot], start=(l != 1), stop=True)
                    mm.then_inc(max_full.sem(run), 1)
                elif kind == "exp":
                    g, kt, h = step[3:]
                    if g % 2 == 0 and kt == 0 and h == 0:
                        max_rows[g // 2].wait(pe, run, step, ("nm", l, s, g // 2))
                    n = exp_full.number(run, step) % 2
                    probs_ready.wait_ago(pe, run, step, 2)
                    for k in range(2):
                        slot = 2 * g + k
                        if l == 1:
                            nc.tensor.matmul(exp_ps[:, n, k], ident_bf[:], bias_kq[:, kt], start=True, stop=False)
                        rows_ = slice(HROWS * h, HROWS * h + K_EXPPASS)
                        mm = nc.tensor.matmul(exp_ps[:, n, k], k_stack[rows_, s, slot, P * kt:P * kt + P],
                                              q_stack[rows_, s, slot], start=(l != 1), stop=True)
                    mm.then_inc(exp_full.sem(run), 1)
                elif kind == "pv":
                    g = step[3]
                    probs_ready.wait(pe, run, step, ("exp", l, s, g, TT - 1, HALVES - 1))
                    if g == 0:
                        if l == 0:
                            pool_v.wait(pe, run, step, ("v", 0, s))
                        else:
                            ready(("v", l, s))
                    n = pv_full.number(run, step) % 2
                    pv_turned.wait_ago(pe, run, step, 2)
                    for kt in range(TT):
                        for j in range(4):
                            h, k = j // 2, j % 2
                            head = SLOTS * h + 2 * g + k
                            mm = nc.tensor.matmul(pv_ps[32 * j:32 * j + 32, n, 0:S],
                                                  v_ones[:, s, kt, head, :], probs[:, g % 2, 4 * h + 2 * kt + k],
                                                  start=(kt == 0), stop=(kt == TT - 1))
                    mm.then_inc(pv_full.sem(run), 1)


        opening = Run(OPENING)
        closing = Run(CLOSING)

        with nc.Block() as block:
            @block.sync
            def _(sp):
                sp.dma_start(ident[:], ident_in).then_inc(s_const, 16)
                sp.dma_start(row[:].rearrange("p r e -> p (r e)"),
                             rows.partition_broadcast(P)).then_inc(s_const, 16)
                sp.dma_start(col[:], cols).then_inc(s_const, 16)
                sp.dma_start(y[:, 0, 0, 0:P], same_slot).then_inc(s_const, 16)
                sp.dma_start(y[:, 0, 0, P:2 * P], same_head).then_inc(s_const, 16)
                sp.dma_start(y[:, 0, 1, 0:P], wv_rep).then_inc(s_const, 16)
                sp.dma_start(z[0:HD, 0, 0:P], wq_rep).then_inc(s_const, 16)
                sp.dma_start(z[0:HD, 0, P:2 * P], wk_rep).then_inc(s_const, 16)
                sp.dma_start(hx[0:B, 0, 0, :].bitcast(I32), mask0).then_inc(s_const, 16)
                sp.dma_start(x_tok[:, :, 0:S // 4].bitcast(I32), mask1.rearrange("(t p) k -> p t k", p=P)).then_inc(s_const, 16)
                sp.dma_start(attn[:], w_out.rearrange("(t p) e -> p t e", p=P)).then_inc(s_const, 16)
                for l in range(2):
                    sp.dma_start(o_w[:, l + 1], wo[l].rearrange("(t p) e -> p t e", p=P)).then_inc(s_const, 16)
                    sp.dma_start(ff2_w[:, l], wff2[l].rearrange("(t p) e -> p t e", p=P)).then_inc(s_const, 16)
                for n, (_, _, src, k, _) in enumerate(splits):
                    if n >= 2:
                        sp.wait_ge(s_lo, n - 1)
                    w = k * src.shape[1]
                    sp.dma_start(stage[:, n % 2, 0:w].rearrange("p (t e) -> p t e", t=k),
                                 src.rearrange("(t p) e -> p t e", p=P)).then_inc(s_raw[n % 2], 16)
                sp.wait_ge(s_dve, 7)
                sp.dma_start(masks_dram[0:B], hx[0:B, 0, 1, :]).then_inc(s_const, 16)
                sp.dma_start(masks_dram[B:B + 1], z[0:1, 1, :]).then_inc(s_const, 16)
                for s in range(LANES):
                    for h in range(HALVES):
                        sp.dma_start(q_stack[HROWS * h:HROWS * h + 1, s].bitcast(F32), hid[0:1, 0:SLOTS, :]).then_inc(s_const, 16)
                        sp.dma_start(k_stack[HROWS * h + R_MAX:HROWS * h + R_MAX + 2, s].bitcast(F32),
                                     hid[0:2, 0:SLOTS, :]).then_inc(s_const, 16)
                sp.wait_ge(s_const, 16 * SETUP_DMAS)
                sp.wait_ge(primed, 1)
                sp.wait_ge(s_act, SETUP_ACT)
                sp.wait_ge(s_dve, SETUP_DVE)

                sync_steps(sp, opening)
                finish_dmas(sp, opening)

            @block.gpsimd
            def _(pool):
                for sg in every:
                    pool.sem_inc(sg.sems[1], sg.per)
                pool.sem_inc(primed, 1)
                pool.wait_ge(s_act, SETUP_ACT)
                pool.wait_ge(s_dve, SETUP_DVE)
                pool.wait_ge(s_const, 16 * SETUP_DMAS)

                pool_steps(pool, opening)

            @block.scalar
            def _(act):
                for n, (hi, _, src, k, scale) in enumerate(splits):
                    act.wait_ge(s_raw[n % 2], 16 * (n // 2 + 1))
                    nc.scalar.activation(hi, stage[:, n % 2, 0:k * src.shape[1]], ACT.Copy, scale=scale).then_inc(s_hi, 1)
                act.wait_ge(s_pe, 1)
                nc.scalar.activation(o_w[:, 0], dense_ps[:, 1], ACT.Copy).then_inc(s_act, 1)
                act.wait_ge(s_pe, 2)
                nc.scalar.activation(bias_kq[:], max_ps[:, 0], ACT.Copy).then_inc(s_act, 1)
                act.wait_ge(primed, 1)
                act.wait_ge(s_dve, SETUP_DVE)

                scalar_steps(act, opening)

            @block.vector
            def _(dve):
                waits = [0]

                def chain(ins):
                    waits[0] += 1
                    ins.then_inc(s_dve, 1)
                    dve.wait_ge(s_dve, waits[0])
                chain(nc.vector.memset(hid[:], 1.0))
                chain(nc.vector.memset(v_ones[:], 1.0))
                chain(nc.vector.memset(nm_tok[:], 0.0))
                chain(nc.vector.memset(minus_half[:], -0.5))
                chain(nc.vector.memset(z[0:1, 1, :], 0.0))
                dve.wait_ge(s_const, 16 * SETUP_LOADS)
                chain(nc.vector.tensor_copy(hx[0:B, 0, 1, :], hx[0:B, 0, 0, :].bitcast(I32)))
                chain(nc.vector.tensor_scalar(hx[0:B, 0, 1, :].bitcast(F32R), hx[0:B, 0, 1, :], 0.0, L0_MASKED,
                                              ALU.is_equal, ALU.mult))
                chain(nc.vector.tensor_copy(ctx_tok[:], x_tok[:].bitcast(U8)[:, :, 0:S]))
                chain(nc.vector.tensor_scalar(ctx_tok[:], ctx_tok[:], 0.0, L1_MASKED, ALU.is_equal, ALU.mult))
                chain(nc.vector.tensor_copy(bias_qk[:], ctx_tok[:]))
                chain(nc.vector.tensor_copy(ident_bf[:], ident[:]))
                chain(nc.vector.tensor_reduce(nan_col[:], ctx_tok[:], AX.X, ALU.max))
                chain(nc.vector.tensor_scalar(nan_col[:], nan_col[:], 1e30, None, ALU.mult))
                chain(nc.vector.tensor_tensor(nan_col[:], nan_col[:], nan_col[:], ALU.subtract))
                chain(nc.vector.tensor_scalar(col[:, C_Q:C_Q + 4], col[:, C_Q:C_Q + 4], 0.25, None, ALU.mult))
                chain(nc.vector.tensor_tensor(y[:, 0, 1, 0:P], y[:, 0, 1, 0:P], y[:, 0, 0, P:2 * P], ALU.mult))
                dve.wait_ge(s_pe, 1)
                chain(nc.vector.scalar_tensor_tensor(q0_w[:], dense_ps[:, 0, 0, 0:P], 1.0 / 16.0, y[:, 0, 0, 0:P],
                                                     ALU.mult, ALU.mult))
                assert waits[0] == SETUP_DVE_CHAIN, waits[0]
                for n, (hi, lo, src, k, scale) in enumerate(splits):
                    dve.wait_ge(s_hi, n + 1)
                    nc.vector.scalar_tensor_tensor(lo, stage[:, n % 2, 0:k * src.shape[1]], scale, hi.bitcast(F32),
                                                   ALU.mult, ALU.subtract).then_inc(s_lo, 1)
                dve.wait_ge(s_lo, len(splits))
                dve.sem_inc(s_dve, 1)
                dve.wait_ge(s_act, SETUP_ACT)
                dve.wait_ge(primed, 1)
                dve.wait_ge(s_const, 16 * SETUP_DMAS)

                vector_steps(dve, opening)

            @block.tensor
            def _(pe):
                pe.wait_ge(s_const, 16 * SETUP_LOADS)
                pe.wait_ge(s_dve, SETUP_DVE_CHAIN - 1)
                nc.tensor.matmul(dense_ps[:, 0, 0, 0:P], z[0:HD, 0, 0:P], z[0:HD, 0, P:2 * P], start=True, stop=True)
                for t in range(FT):
                    last = nc.tensor.matmul(dense_ps[:, 1, t], y[:, 0, 1, 0:P], attn[:, t], start=True, stop=True)
                last.then_inc(s_pe, 1)
                for kt in range(TT):
                    for t in range(TT):
                        last = nc.tensor.transpose(max_ps[:, 0, kt, P * t:P * t + P], ctx_tok[:, t, P * kt:P * kt + P],
                                                   ident[:])
                last.then_inc(s_pe, 1)
                pe.wait_ge(s_act, SETUP_ACT)
                pe.wait_ge(s_dve, SETUP_DVE)
                pe.wait_ge(s_const, 16 * SETUP_DMAS)
                pe.wait_ge(primed, 1)

                tensor_steps(pe, opening)

        with nc.Block() as block:
            @block.sync
            def _(sp):
                with sp.Fori(0, N_LOOP) as i:
                    sync_steps(sp, Run(LOOP, i))
                finish_dmas(sp, Run(LOOP, 0))

            @block.gpsimd
            def _(pool):
                with pool.Fori(0, N_LOOP) as i:
                    pool_steps(pool, Run(LOOP, i))

            @block.scalar
            def _(act):
                with act.Fori(0, N_LOOP) as i:
                    scalar_steps(act, Run(LOOP, i))

            @block.vector
            def _(dve):
                with dve.Fori(0, N_LOOP) as i:
                    vector_steps(dve, Run(LOOP, i))

            @block.tensor
            def _(pe):
                with pe.Fori(0, N_LOOP) as i:
                    tensor_steps(pe, Run(LOOP, i))

        with nc.Block() as block:
            @block.sync
            def _(sp):
                sync_steps(sp, closing)
                finish_dmas(sp, closing)

            @block.gpsimd
            def _(pool):
                pool_steps(pool, closing)

            @block.scalar
            def _(act):
                scalar_steps(act, closing)

            @block.vector
            def _(dve):
                vector_steps(dve, closing)

            @block.tensor
            def _(pe):
                tensor_steps(pe, closing)


def kernel(**inputs):
    import numpy as _np
    import concourse.bacc as _bacc
    from concourse import mybir as _mybir
    from concourse.bass_utils import run_bass_kernel_spmd as _run

    a = {k: _np.asarray(v) for k, v in inputs.items()}
    f, s, d, g, j = 2, 8, 16, 4, 2
    nat = _np.arange(256)
    ds = nat.reshape(f, s, d).transpose(0, 2, 1).reshape(-1)
    comp = nat.reshape(f, g, j, d).transpose(0, 2, 3, 1).reshape(-1)
    L0, L1 = "L0_xattn_", "L1_xattn_"

    def tiles(v):
        return v.reshape(-1, 128).T

    ins = {
        "x": a["x"],
        "ctx_in": a["ctx_1024"][:, :, ds],
        "mask0": a["mask_Bx1x1xS2_if1"].reshape(16, 256),
        "mask1": a["mask_1x1xSxS_bk0"].reshape(256, 256).view(_np.int32),
        "wq_rep": _np.tile(a[L0 + "wq"].T, (1, s)),
        "wk_rep": _np.repeat(a[L0 + "wk"].T, s, axis=1),
        "wv_rep": _np.tile(_np.repeat(_np.repeat(a[L0 + "wv"].T, g, 0), g, 1), (j, j)),
        "w_out": a[L0 + "w_out"][comp],
        "wq1": a[L1 + "sa_wq"][:, ds], "wk1": a[L1 + "sa_wk"][:, ds], "wv1": a[L1 + "sa_wv"],
        "wq2": a[L1 + "ca_wq"][:, ds], "wk2": a[L1 + "ca_wk"][ds][:, ds], "wv2": a[L1 + "ca_wv"][ds],
        "wo1": a[L1 + "sa_wo"][comp], "wo2": a[L1 + "ca_wo"][comp],
        "wf1_0": a[L0 + "w_ff1"], "wf1_1": a[L1 + "ff_w1"],
        "wf2_0": a[L0 + "w_ff2"], "wf2_1": a[L1 + "ff_w2"],
        "rows": _np.stack([a[L0 + "g1"], a[L0 + "beta1"], a[L0 + "g2"], a[L0 + "beta2"],
                           a[L1 + "ln1_g"], a[L1 + "ln1_b"], a[L1 + "ln2_g"], a[L1 + "ln2_b"],
                           a[L1 + "ln3_g"], a[L1 + "ln3_b"],
                           a[L0 + "b_out"], a[L0 + "b_ff2"], a[L1 + "sa_bo"], a[L1 + "ca_bo"], a[L1 + "ff_b2"],
                           a[L1 + "sa_bv"], a[L1 + "ca_bv"]]).reshape(-1),
        "cols": _np.concatenate([tiles(a[L1 + "sa_bq"][ds]), tiles(a[L1 + "ca_bq"][ds]), tiles(a[L1 + "sa_bk"][ds]),
                                 tiles(a[L1 + "ca_bk"][ds]), tiles(a[L0 + "b_ff1"]), tiles(a[L1 + "ff_b1"])], 1),
    }
    slot_k, slot_m = nat[:128] // d, nat[:128] % s
    head = (nat[:128] // 64) * g + nat[:128] % g
    ins["ident"] = _np.eye(128, dtype=_np.float32)
    ins["same_slot"] = (slot_k[:, None] == slot_m[None, :]).astype(_np.float32)
    ins["same_head"] = (head[:, None] == head[None, :]).astype(_np.float32)

    nc = _bacc.Bacc("TRN2", target_bir_lowering=False, num_devices=1, dynamic_dma_scratch_size=1024)
    arrays, ap = {}, {}
    for name, v in ins.items():
        arrays[f"in_{name}"] = _np.ascontiguousarray(v)
        ap[name] = nc.dram_tensor(f"in_{name}", v.shape, _mybir.dt.from_np(v.dtype), kind="ExternalInput").ap()
    out = nc.dram_tensor("out_0", (16, 256, 256), _mybir.dt.float32, kind="ExternalOutput").ap()
    masks = nc.dram_tensor("masks_dram", (17, 256), _mybir.dt.float32, kind="Internal").ap()
    build(nc, ap["x"], ap["ctx_in"], ap["mask0"], ap["mask1"], ap["wq_rep"], ap["wk_rep"], ap["wv_rep"], ap["w_out"],
          [ap[n] for n in ("wq1", "wk1", "wv1", "wq2", "wk2", "wv2")], [ap["wo1"], ap["wo2"]],
          [ap["wf1_0"], ap["wf1_1"]], [ap["wf2_0"], ap["wf2_1"]], ap["rows"], ap["cols"], ap["ident"],
          ap["same_slot"], ap["same_head"], out, masks)
    r = _run(nc, [arrays], core_ids=[0])
    return r.results[0]["out_0"]
```

```python
from contextlib import ExitStack

import concourse.bass as bass
from concourse import mybir

ALU = mybir.AluOpType
ACT = mybir.ActivationFunctionType
AX = mybir.AxisListType
F32 = mybir.dt.float32
F32R = mybir.dt.float32r
BF16 = mybir.dt.bfloat16
I32 = mybir.dt.int32
U8 = mybir.dt.uint8

P = 128
B, S, E = 16, 256, 256
H, HD = 16, 16
FF = 1024
LANES = 2
NI = B // LANES
FT = E // P
TT = S // P
NF = FF // P
HALVES, SLOTS = 2, 8
GROUPS = 4
HROWS = 64
R_MASK, R_A, R_B, R_C, R_MAX = 0, 1, 17, 33, 49
K_MAXPASS, K_EXPPASS = 49, 51
EPS = 1e-5
L0_MASKED = -1e20 / 16.0
L1_MASKED = -1e30
ROWS = ["g0", "be0", "g1", "be1", "g2", "be2", "g3", "be3", "g4", "be4",
        "b_res0", "b_ff0", "b_o1", "b_o2", "b_ff1", "bv1", "bv2"]
RI = {n: i for i, n in enumerate(ROWS)}
C_Q, C_K, C_F = 0, 4, 8
NCOLS = 8 + 2 * NF
COSTS = {
    "load": [("sync", 0.84), ("wire", 4.40)], "r0": [("sync", 1.22), ("wire", 2.52)],
    "stq": [("sync", 3.56), ("wire", 2.52)], "stk": [("sync", 3.56), ("wire", 2.52)],
    "tc": [("tensor", 0.39), ("scalar", 0.62), ("vector", 0.62)], "tx": [("tensor", 0.39), ("scalar", 0.62)],
    "th": [("tensor", 0.39), ("scalar", 0.62), ("vector", 0.62)],
    "q": [("tensor", 1.29), ("scalar", 0.93), ("vector", 0.79)],
    "k": [("tensor", 1.29), ("scalar", 0.93), ("vector", 0.79)], "v": [("tensor", 1.29), ("vector", 0.70)],
    "v0": [("gpsimd", 2.3)], "rx": [("gpsimd", 1.5)], "max": [("tensor", 0.30), ("vector", 0.57)],
    "ng": [("vector", 0.53)], "nm": [("tensor", 0.2), ("scalar", 0.41), ("sync", 1.22), ("wire", 2.52)],
    "exp": [("tensor", 0.30), ("scalar", 0.57)], "pv": [("tensor", 1.21), ("vector", 1.05)],
    "oc": [("vector", 0.62), ("sync", 2.34), ("wire", 2.52)], "o": [("tensor", 1.42), ("vector", 0.62)],
    "ls": [("vector", 0.97), ("gpsimd", 1.0)], "ln": [("vector", 1.58)], "rs": [("gpsimd", 1.5)],
    "ff1": [("tensor", 1.16), ("scalar", 0.93)], "ff2": [("tensor", 5.16), ("vector", 0.62)],
    "store": [("sync", 0.47), ("wire", 3.77)]}
HELD = [(("max0",), ("nm0",), 1), (("max1",), ("nm1",), 1), (("exp",), ("oc",), 1),
        (("tx", "ff1"), ("q", "ff2"), 1), (("q",), ("stq",), 1), (("k",), ("stk",), 1), (("load",), ("rx",), 2)]
TAIL_WEIGHT = 2.0
LAG = 2

SETUP_LOADS, SETUP_PLAIN, SETUP_DMAS = 11, 4, 21
SETUP_ACT = 2
SETUP_DVE_CHAIN = 16
SETUP_DVE = SETUP_DVE_CHAIN + 1


def needed(x):
    kind, l, s = x[:3]
    if kind in ("tc", "tx", "v0"):
        return [("load", 0, s)]
    if kind == "rx":
        return [("v0", 0, s)]
    if kind == "th":
        return [("ln", (0, 2, 3, 4)[l], s)]
    if kind == "q":
        return [("th", l, s) if l else ("tx", 0, s)]
    if kind in ("k", "v"):
        return [("th", 1, s)] if l == 1 else [("tc", 0, s)]
    if kind == "stq":
        return [("q", l, s)]
    if kind == "stk":
        return [("k", l, s) if l else ("tc", 0, s)]
    if kind == "max":
        return [("stq", l, s), ("stk", l, s)] + ([("r0", l, s)] if l < 2 else [])
    if kind == "ng":
        return [("max", l, s, x[3], TT - 1, 1, HALVES - 1)]
    if kind == "nm":
        return [("ng", l, s, x[3])]
    if kind == "exp":
        return [("nm", l, s, x[3] // 2)]
    if kind == "pv":
        return [("exp", l, s, x[3], TT - 1, HALVES - 1), ("v", l, s) if l else ("v0", 0, s)]
    if kind == "oc":
        return [("pv", l, s, GROUPS - 1)]
    if kind == "o":
        return [("oc", l, s), [("rx", 0, s), ("rs", 1, s), ("rs", 3, s)][l]]
    if kind == "ls":
        return [(("o", 0, s), ("ff2", 0, s), ("ln", 1, s), ("o", 1, s), ("o", 2, s))[l]]
    if kind == "ln":
        return [("ls", l, s)]
    if kind == "rs":
        return [(("ln", 0, s), ("ln", 1, s), None, ("o", 1, s), ("o", 2, s))[l]]
    if kind == "ff1":
        return [("th", 3 * l, s)]
    if kind == "ff2":
        return [("ff1", l, s, NF // 2 - 1)]
    return [("ff2", 1, s)] if kind == "store" else []


def is_dense(x):
    return x[0] in ("tx", "tc", "q", "k", "v", "nm", "o", "th", "ff1", "ff2")


def name(x):
    return f"{x[0]}{x[3]}" if x[0] in ("max", "nm") else x[0]


def merge(streams):
    clock, done, ring, owner, out = {}, {}, {}, {}, []
    streams = [list(steps) for steps in streams]
    pending = {y for steps in streams for y in steps}
    left = [sum(us for x, m in steps for engine, us in COSTS[x[0]]) for steps in streams]

    def ring_of(x):
        return "dense" if is_dense(x) else x[0]

    def start(x, m, who):
        needs = [(y, m) for y in needed(x)]
        if any(y in pending for y in needs):
            return None
        if any(name(x) in first and owner.get(n, who // by) != who // by for n, (first, last, by) in enumerate(HELD)):
            return None
        waits = [done.get(y, 0.0) for y in needs] + [clock.get(COSTS[x[0]][0][0], 0.0)]
        return max(waits + [ring.get(ring_of(x), (0.0, 0.0))[0]])

    while pending:
        heads = [(start(*steps[0], who), -left[who] * (TAIL_WEIGHT if who % 2 else 1.0), who)
                 for who, steps in enumerate(streams) if steps and start(*steps[0], who) is not None]
        now, _, who = min(heads)
        x, m = streams[who].pop(0)
        for n, (first, last, by) in enumerate(HELD):
            if name(x) in first:
                owner[n] = who // by
            if name(x) in last and owner.get(n) == who // by:
                del owner[n]
        for engine, us in COSTS[x[0]]:
            now = max(now + 0.10, clock.get(engine, 0.0) if engine != "wire" else 0.0) + us
            clock[engine] = now
            left[who] -= us
        done[x, m] = now
        if ring_of(x) in ("dense", "max", "exp", "pv"):
            ring[ring_of(x)] = (ring.get(ring_of(x), (0.0, 0.0))[1], now)
        pending.discard((x, m))
        out.append((x, m))
    return out


def attend(l, s):
    def maxes(hs):
        return [("max", l, s, hs, t, sp, h) for t in range(TT) for sp in range(2) for h in range(HALVES)]

    exps = [("exp", l, s, g, kt, h) for g in range(GROUPS) for kt in range(TT) for h in range(HALVES)]
    for g in range(GROUPS - 1):
        exps.insert(5 * g + 4 + LAG, ("pv", l, s, g))
    second = maxes(1)
    beside = [*second[6:], ("ng", l, s, 1), None, None, ("nm", l, s, 1)] + [None] * len(exps)
    mixed = [x for pair in zip(exps, beside) for x in pair if x]
    return (maxes(0) + [("ng", l, s, 0)] + second[:3] + [("nm", l, s, 0)] + second[3:6] + mixed
            + [("pv", l, s, GROUPS - 1), ("oc", l, s)])


def ffn(f, s):
    return [("ff1", f, s, c) for c in range(NF // 2)] + [("ff2", f, s)]


def chain(s, m):
    def of(*steps):
        return [(x, m) for x in steps]
    start = [("tc", 0, s), ("r0", 0, s), ("stk", 0, s), ("tx", 0, s), ("q", 0, s), ("stq", 0, s), ("v0", 0, s)]
    after0 = [("o", 0, s), ("ls", 0, s), ("ln", 0, s), ("rs", 0, s), ("th", 0, s)] + ffn(0, s)
    before1 = [("ls", 1, s), ("ln", 1, s), ("ls", 2, s), ("rs", 1, s), ("ln", 2, s), ("th", 1, s), ("r0", 1, s),
               ("k", 1, s), ("stk", 1, s), ("q", 1, s), ("stq", 1, s), ("v", 1, s)]
    between = [("k", 2, s), ("stk", 2, s), ("v", 2, s), ("o", 1, s), ("ls", 3, s), ("rs", 3, s), ("ln", 3, s),
               ("th", 2, s), ("q", 2, s), ("stq", 2, s)]
    after2 = [("o", 2, s), ("ls", 4, s), ("rs", 4, s), ("ln", 4, s), ("th", 3, s)]
    return (of(*start), of(*attend(0, s), *after0, *before1, *attend(1, s), *between, *attend(2, s)), of(*after2))


def lane_streams(s, turns):
    main, tail = [(("load", 0, s), 0)], [(("rx", 0, s), 0)]
    for m in range(turns):
        start, body, after2 = chain(s, m)
        if m == 0:
            main += start
        main += body
        if m + 1 < turns:
            nxt = chain(s, m + 1)[0]
            cut = len(main) - 15
            main = main[:cut] + [(("load", 0, s), m + 1)] + main[cut:]
            main += nxt[:4] + after2[:1] + nxt[4:] + after2[1:]
        else:
            main += after2
        tail += [(x, m) for x in ffn(1, s) + [("store", 0, s)]]
        if m + 1 < turns:
            tail.append((("rx", 0, s), m + 1))
    return [main, tail]


def steady_order():
    order = merge([stream for s in range(LANES) for stream in lane_streams(s, 7)])
    first = ("max", 2, 0, 0, 0, 0, 0)
    begin, end = order.index((first, STEADY)), order.index((first, STEADY + 1))
    ahead = {x: m - STEADY for x, m in order[begin:end]}
    steps = [x for x, m in order[begin:end]]
    assert len(set(steps)) == len(steps) == len({x for x, m in order}), "not periodic"
    assert set(ahead.values()) == {0, 1}
    return steps, ahead


STEADY = 3
LOOP, AHEAD = steady_order()
N_LOOP = NI - 1
OPENING = [x for x, m in merge([[(x, m) for x, m in stream if m == 0 and AHEAD[x]] for s in range(LANES)
                                for stream in lane_streams(s, 1)])]
CLOSING = [x for x, m in merge([[(x, m) for x, m in stream if not AHEAD[x]] for s in range(LANES)
                                for stream in lane_streams(s, 1)])]
PEELED = OPENING + CLOSING


class Run:

    def __init__(self, steps, i=None):
        self.steps, self.i, self.looped = steps, i, int(i is not None)
        self.at = {x: n for n, x in enumerate(LOOP if self.looped else PEELED)}

    def sequence_number(self, step):
        if self.looped:
            return self.i * LANES + (step[2] + LANES * AHEAD[step])
        return step[2] if AHEAD[step] else B - LANES + step[2]


class Signal:

    def __init__(self, peeled, in_loop, steps, inc):
        self.sems, self.inc, self.steps = (peeled, in_loop), inc, steps
        self.order = tuple({x: n + 1 for n, x in enumerate(seq)} for seq in steps)
        self.per = inc * len(steps[1])

    def number(self, run, x):
        return self.order[run.looped][x] - 1

    def sem(self, run):
        return self.sems[run.looped]

    def await_count(self, eng, run, count):
        if run.looped:
            eng.wait_ge(self.sems[1], run.i * self.per + (self.per + count))
        elif count > 0:
            eng.wait_ge(self.sems[0], count)

    def wait(self, eng, run, step, x=None, part=0):
        x = x or step
        count = self.order[run.looped][x] * self.inc - (self.inc - part if part else 0)
        if run.at[x] > run.at[step]:
            count -= self.per if run.looped else count
        self.await_count(eng, run, count)

    def wait_last(self, eng, run, step, chosen=lambda x: True):
        found = [x for x in self.steps[run.looped] if chosen(x)]
        ahead = [x for x in found if run.at[x] < run.at[step]]
        if ahead:
            self.await_count(eng, run, self.order[run.looped][ahead[-1]] * self.inc)
        elif run.looped:
            self.await_count(eng, run, self.order[1][found[-1]] * self.inc - self.per)

    def wait_ago(self, eng, run, x, back=1):
        self.await_count(eng, run, (self.order[run.looped][x] - back) * self.inc)

    def total(self, run):
        if run.looped:
            return self.per * (N_LOOP + 1)
        return self.inc * sum(x in self.order[0] for x in PEELED[:run.at[run.steps[-1]] + 1])


def build(nc, x, ctx_in, mask0, mask1, wq_rep, wk_rep, wv_rep, w_out, wqkv, wo, wff1, wff2, rows, cols, ident_in,
          same_slot, same_head, out, masks_dram):
    every = []

    with ExitStack() as ctx:
        def sb(name, shape, dt=F32):
            return ctx.enter_context(nc.sbuf_tensor(name, shape, dt))

        def sem(name):
            return ctx.enter_context(nc.semaphore(name))

        def signal(name, inc, *chosen):
            picked = chosen if len(chosen) == 2 else [[x for x in seq if chosen[0](x)] for seq in (PEELED, LOOP)]
            every.append(Signal(sem(name + "_once"), sem(name), tuple(picked), inc))
            return every[-1]

        def each_lane(name, inc, chosen):
            return [signal(f"{name}{s}", inc, lambda x, s=s: x[2] == s and chosen(x)) for s in range(LANES)]

        def kinds(*names):
            return lambda x: x[0] in names

        dense_ps = ctx.enter_context(nc.psum_tensor("dense_ps", [P, 2, 2, 256], F32))
        max_ps = ctx.enter_context(nc.psum_tensor("max_ps", [P, 2, 2, 256], F32))
        exp_ps = ctx.enter_context(nc.psum_tensor("exp_ps", [P, 2, 2, 256], F32))
        pv_ps = ctx.enter_context(nc.psum_tensor("pv_ps", [P, 2, 512], F32))

        qkv_w = sb("qkv_w", [P, 6, 2, FT, E], F32R)
        ff1_w = sb("ff1_w", [P, 2, 2, FT, FF], F32R)
        ff2_w = sb("ff2_w", [P, 2, NF, E])
        o_w = sb("o_w", [P, 3, FT, E])
        q0_w = sb("q0_w", [P, P])
        row = sb("row", [P, len(ROWS), E])
        col = sb("col", [P, NCOLS])
        ident = sb("ident", [P, P])
        ident_bf = sb("ident_bf", [P, P], BF16)
        bias_qk = sb("bias_qk", [P, TT, S], BF16)
        bias_kq = sb("bias_kq", [P, TT, S], BF16)
        nan_col = sb("nan_col", [P, TT])
        minus_half = sb("minus_half", [P, TT])

        x_tok = sb("x_tok", [P, TT, E])
        ctx_tok = sb("ctx_tok", [P, TT, E])
        ctxT = sb("ctxT", [P, LANES, 2, FT, S], F32R)
        qT = sb("qT", [P, 2, FT, S], F32R)
        kT = sb("kT", [P, 2, FT, S], F32R)
        q_stack = sb("q_stack", [P, LANES, SLOTS, S], F32R)
        k_stack = sb("k_stack", [P, LANES, SLOTS, S], F32R)
        v_ones = sb("v_ones", [P, LANES, TT, H, 2 * HD])
        m_tok = sb("m_tok", [P, 2, TT, 8])
        nm_tok = sb("nm_tok", [P, 2, TT, P])
        nmT = sb("nmT", [16, 2, S], F32R)
        probs = sb("probs", [P, 2, HALVES * TT * 2, S])
        pv_t = sb("pv_t", [P, 2, S])
        inverse = sb("inverse", [P, 2, S // 32, 1])
        attn_pad = sb("attn_pad", [P, GROUPS, S])
        attn = sb("attn", [P, FT, S])
        res = sb("res", [P, LANES, TT, E])
        y = sb("y", [P, LANES, TT, E])
        z = sb("z", [P, TT, E])
        hx = sb("hx", [P, LANES, TT, E])
        hT = sb("hT", [P, LANES, 2, FT, S], F32R)
        hid = sb("hid", [P, NF, S])
        xT = hid[:, 0:FT, :]
        st = sb("st", [P, LANES, TT, 6])
        mv = sb("mv", [P, LANES, TT, 2])
        rstd = sb("rstd", [P, LANES, TT])
        vare = sb("vare", [P, LANES, TT])

        loaded = each_lane("loaded", 32, kinds("load"))
        dense_full = signal("dense_full", 1, is_dense)
        evacuated = [signal(f"evacuated{b}", 2, dense_full.steps[0][b::2], dense_full.steps[1][b::2])
                     for b in range(2)]
        pool_v = signal("pool_v", 1, kinds("v0"))
        q_stacked = each_lane("q_stacked", 96, kinds("stq"))
        k_stacked = each_lane("k_stacked", 96, kinds("stk"))
        mask_row = each_lane("mask_row", 32, kinds("r0"))
        max_full = signal("max_full", 1, kinds("max"))
        max_taken = signal("max_taken", 1, kinds("max"))
        neg_hi = signal("neg_hi", 2, kinds("ng"))
        neg_lo = signal("neg_lo", 1, kinds("ng"))
        max_rows = [signal(f"max_rows{hs}", 32, lambda x, hs=hs: x[0] == "nm" and x[3] == hs) for hs in range(2)]
        exp_full = signal("exp_full", 1, kinds("exp"))
        probs_ready = signal("probs_ready", 1, kinds("exp"))
        pv_full = signal("pv_full", 1, kinds("pv"))
        pv_turned = signal("pv_turned", 1, kinds("pv"))
        inverted = signal("inverted", 1, kinds("pv"))
        normed = signal("normed", 1, kinds("pv"))
        turned_back = signal("turned_back", 1, kinds("pv"))
        compacted = signal("compacted", 64, kinds("oc"))
        stats_part = signal("stats_part", 1, kinds("ls"))
        stats = signal("stats", 1, kinds("ls"))
        eps_added = signal("eps_added", 1, kinds("ls"))
        rstd_ready = signal("rstd_ready", 1, kinds("ls"))
        scaled = signal("scaled", 1, kinds("ln"))
        ln_done = signal("ln_done", 1, kinds("ln"))
        res_ready = signal("res_ready", 1, kinds("rx", "rs"))
        stored = each_lane("stored", 16, kinds("store"))
        by_dma = [*loaded, *q_stacked, *k_stacked, *mask_row, *max_rows, compacted, *stored]
        assert all(len(sg.steps[1]) % 2 == 0 for sg in (dense_full, max_full, exp_full, pv_full))

        def bank(run, x):
            return dense_full.number(run, x) % 2

        def evac(run, x):
            return evacuated[bank(run, x)]

        def product(run, x):
            return dense_ps[:, bank(run, x)]

        primed = sem("primed")
        s_const = sem("s_const")
        s_plain = sem("s_plain")
        s_raw = [sem(f"s_raw{n}") for n in range(9)]
        s_hi = sem("s_hi")
        s_lo = sem("s_lo")
        s_dve = sem("s_dve")
        s_pe = sem("s_pe")
        s_act = sem("s_act")
        carrier = sem("carrier")
        carrier_sp = sem("carrier_sp")
        carrier_dve = sem("carrier_dve")

        splits = []
        for n in range(6):
            splits.append((qkv_w[:, n, 0].rearrange("p k e -> p (k e)"), qkv_w[:, n, 1].rearrange("p k e -> p (k e)"),
                           wqkv[n], FT, 0.25 if n % 3 == 0 else 1.0,
                           probs[:, n // 4].rearrange("p b e -> p (b e)")[:, FT * E * (n % 4):FT * E * (n % 4 + 1)]))
        splits.append((ff1_w[:, 0, 0].rearrange("p k e -> p (k e)"), ff1_w[:, 0, 1].rearrange("p k e -> p (k e)"),
                       wff1[0], FT, 1.0, hid[:].rearrange("p k e -> p (k e)")))
        for k, place in enumerate((attn_pad[:].rearrange("p g e -> p (g e)"),
                                   res[:].rearrange("p s t e -> p (s t e)"))):
            splits.append((ff1_w[:, 1, 0, k], ff1_w[:, 1, 1, k], wff1[1][P * k:P * k + P], 1, 1.0, place))

        def sync_steps(sp, run):
            def hold():
                sp.sem_inc(carrier_sp, 1)

            for step in run.steps:
                kind, l, s = step[:3]
                if kind == "load":
                    dense_full.wait_last(sp, run, step, kinds("tx"))
                    hold()
                    pool_v.wait_last(sp, run, step)
                    hold()
                    res_ready.wait_last(sp, run, step, kinds("rx"))
                    hold()
                    b = run.sequence_number(step)
                    sp.dma_start(ctx_tok[:], ctx_in[bass.ds(b, 1)].rearrange("a (t p) e -> p (a t) e", p=P)
                                 ).then_inc(loaded[s].sem(run), 16)
                    sp.dma_start(x_tok[:], x[bass.ds(b, 1)].rearrange("a (t p) e -> p (a t) e", p=P)
                                 ).then_inc(loaded[s].sem(run), 16)
                elif kind == "r0":
                    exp_full.wait_last(sp, run, step, lambda x: x[2] == s)
                    hold()
                    src = masks_dram[bass.ds(run.sequence_number(step), 1)] if l == 0 else masks_dram[B:B + 1]
                    for h in range(HALVES):
                        sp.dma_start(k_stack[HROWS * h:HROWS * h + 1, s].bitcast(F32),
                                     src.rearrange("a (o k) -> a o k", o=1).to_broadcast([1, SLOTS, S])
                                     ).then_inc(mask_row[s].sem(run), 16)
                elif kind in ("stq", "stk"):
                    key = ("q" if kind == "stq" else "k", l, s)
                    if kind == "stk" and l == 0:
                        key = ("tc", 0, s)
                    evac(run, key).wait(sp, run, step, key, part=1)
                    hold()
                    exp_full.wait_last(sp, run, step, lambda x: x[2] == s)
                    hold()
                    sg = (q_stacked if kind == "stq" else k_stacked)[s]
                    dst, r_high, r_low = (q_stack, (R_A, R_B), R_C) if kind == "stq" else (k_stack, (R_A, R_C), R_B)
                    for r, part in [(r_high[0], 0), (r_high[1], 0), (r_low, 1)]:
                        if part == 1:
                            evac(run, key).wait(sp, run, step, key)
                            hold()
                        for h in range(HALVES):
                            src = (qT if kind == "stq" else kT)[:, part, h, :]
                            if kind == "stk" and l == 0:
                                src = ctxT[:, s, part, h, :]
                            sp.dma_start(dst[HROWS * h + r:HROWS * h + r + HD, s].bitcast(F32), src.bitcast(F32)
                                         ).then_inc(sg.sem(run), 16)
                elif kind == "nm":
                    hs = step[3]
                    evac(run, step).wait(sp, run, step)
                    hold()
                    exp_full.wait_last(sp, run, step, lambda x: x[2] == s and x[3] // 2 == hs)
                    hold()
                    for h in range(HALVES):
                        sp.dma_start(q_stack[HROWS * h + R_MAX:HROWS * h + R_MAX + 2, s, 4 * hs:4 * hs + 4
                                             ].bitcast(F32),
                                     nmT[8 * h:8 * h + 8, hs, :].bitcast(F32)).then_inc(max_rows[hs].sem(run), 16)
                elif kind == "oc":
                    turned_back.wait(sp, run, step, ("pv", l, s, GROUPS - 1))
                    hold()
                    dense_full.wait_last(sp, run, step, kinds("o"))
                    hold()
                    for j in range(4):
                        sp.dma_start(attn[64 * (j % 2):64 * (j % 2) + 64, j // 2, :],
                                     attn_pad[32 * j:32 * j + HD]).then_inc(compacted.sem(run), 16)
                elif kind == "store":
                    evac(run, ("ff2", 1, s)).wait(sp, run, step, ("ff2", 1, s))
                    hold()
                    b = run.sequence_number(step)
                    sp.dma_start(out[bass.ds(b, 1)].rearrange("a (t p) e -> p (a t) e", p=P), y[:, s]
                                 ).then_inc(stored[s].sem(run), 16)

        def finish_dmas(sp, run):
            for sg in by_dma:
                sp.wait_ge(sg.sem(run), sg.total(run))

        def pool_steps(pool, run):
            def hold():
                pool.sem_inc(carrier, 1)

            for step in run.steps:
                kind, l, s = step[:3]
                if kind == "v0":
                    loaded[s].wait(pool, run, step, ("load", 0, s))
                    hold()
                    pv_full.wait_last(pool, run, step, lambda x: x[2] == s)
                    hold()
                    for t in range(TT):
                        for h in range(HALVES):
                            last = nc.gpsimd.tensor_copy(
                                v_ones[:, s, t, SLOTS * h:SLOTS * h + SLOTS, 0:HD],
                                ctx_tok[:, t, P * h:P * h + P].rearrange("p (d s) -> p s d", d=HD))
                    last.then_inc(pool_v.sem(run), 1)
                elif kind == "rx":
                    evac(run, ("ff2", 1, s)).wait(pool, run, step, ("ff2", 1, s))
                    hold()
                    loaded[s].wait(pool, run, step, ("load", 0, s))
                    hold()
                    for t in range(TT):
                        last = nc.gpsimd.tensor_tensor(res[:, s, t], x_tok[:, t], row[:, RI["b_res0"]], ALU.add)
                    last.then_inc(res_ready.sem(run), 1)
                elif kind == "ls":
                    stats.wait(pool, run, step)
                    hold()
                    nc.gpsimd.tensor_scalar(vare[:, s], mv[:, s, :, 1], EPS, None, ALU.add
                                            ).then_inc(eps_added.sem(run), 1)
                    eps_added.wait(pool, run, step)
                    nc.gpsimd.tensor_tensor(rstd[:, s], vare[:, s], minus_half[:], ALU.pow
                                            ).then_inc(rstd_ready.sem(run), 1)
                elif kind == "rs":
                    if l < 2:
                        ln_done.wait(pool, run, step, ("ln", l, s))
                    else:
                        evac(run, ("o", l - 2, s)).wait(pool, run, step, ("o", l - 2, s))
                    hold()
                    src = hx if l == 0 else y
                    b = {0: "b_ff0", 1: "b_o1", 3: "b_o2", 4: "b_ff1"}[l]
                    for t in range(TT):
                        last = nc.gpsimd.tensor_tensor(res[:, s, t], src[:, s, t], row[:, RI[b]], ALU.add)
                    last.then_inc(res_ready.sem(run), 1)

        def scalar_steps(act, run):
            for step in run.steps:
                kind, l, s = step[:3]
                if is_dense(step) and kind not in ("v", "o", "ff2"):
                    d = product(run, step)
                    ev = evac(run, step).sem(run)
                    dense_full.wait(act, run, step)
                if kind == "tc":
                    k_stacked[s].wait_last(act, run, step)
                    nc.scalar.activation(ctxT[:, s, 0], d, ACT.Copy).then_inc(ev, 1)
                elif kind == "tx":
                    nc.scalar.activation(xT, d, ACT.Copy).then_inc(ev, 2)
                elif kind in ("q", "k"):
                    for sg in q_stacked if kind == "q" else k_stacked:
                        sg.wait_last(act, run, step, lambda x: kind == "q" or x[1] > 0)
                    dst = (qT if kind == "q" else kT)
                    if l == 0:
                        nc.scalar.activation(dst[:, 0], d, ACT.Copy).then_inc(ev, 1)
                    else:
                        c = (C_Q if kind == "q" else C_K) + (l - 1) * FT
                        for f in range(FT):
                            last = nc.scalar.activation(dst[:, 0, f], d[:, f], ACT.Identity,
                                                        bias=col[:, c + f:c + f + 1])
                        last.then_inc(ev, 1)
                elif kind == "nm":
                    max_rows[step[3]].wait_ago(act, run, step)
                    nc.scalar.activation(nmT[:, step[3]], d.rearrange("p a q -> p (a q)")[0:16, 0:S], ACT.Copy
                                         ).then_inc(ev, 2)
                elif kind == "th":
                    nc.scalar.activation(hT[:, s, 0], d, ACT.Copy).then_inc(ev, 1)
                elif kind == "ff1":
                    for f in range(2):
                        m = 2 * step[3] + f
                        c = C_F + l * NF + m
                        last = nc.scalar.activation(hid[:, m], d[:, f], ACT.Relu, bias=col[:, c:c + 1])
                    last.then_inc(ev, 2)
                elif kind == "exp":
                    g, kt, h = step[3:]
                    exp_full.wait(act, run, step)
                    if kt == 0 and h == 0:
                        pv_full.wait_ago(act, run, ("pv", l, s, g), 2)
                    nc.scalar.activation(probs[:, g % 2, 4 * h + 2 * kt:4 * h + 2 * kt + 2],
                                         exp_ps[:, exp_full.number(run, step) % 2], ACT.Exp
                                         ).then_inc(probs_ready.sem(run), 1)

        def vector_steps(dve, run):
            def hold():
                dve.sem_inc(carrier_dve, 1)

            def normalise(x):
                n = pv_full.number(run, x) % 2
                inverted.wait(dve, run, step, x)
                blocks = pv_t[:, n].rearrange("p (b r) -> p b r", r=32)
                nc.vector.tensor_tensor(blocks[:, :, 0:HD], blocks[:, :, 0:HD],
                                        inverse[:, n].to_broadcast([P, S // 32, HD]), ALU.mult
                                        ).then_inc(normed.sem(run), 1)

            def turn_back(x):
                if x[3] == 0:
                    compacted.wait_last(dve, run, step)
                    hold()
                normed.wait(dve, run, step, x)
                nc.vector.transpose(attn_pad[:, x[3]], pv_t[:, pv_full.number(run, x) % 2]
                                    ).then_inc(turned_back.sem(run), 1)

            for step in run.steps:
                kind, l, s = step[:3]
                if is_dense(step):
                    d = product(run, step)
                    ev = evac(run, step)
                if kind == "tc":
                    ev.wait(dve, run, step, part=1)
                    nc.vector.tensor_tensor(ctxT[:, s, 1], d, ctxT[:, s, 0].bitcast(F32), ALU.subtract
                                            ).then_inc(ev.sem(run), 1)
                elif kind in ("q", "k"):
                    ev.wait(dve, run, step, part=1)
                    dst = qT if kind == "q" else kT
                    if l == 0:
                        nc.vector.tensor_tensor(dst[:, 1], d, dst[:, 0].bitcast(F32), ALU.subtract
                                                ).then_inc(ev.sem(run), 1)
                    else:
                        c = (C_Q if kind == "q" else C_K) + (l - 1) * FT
                        for f in range(FT):
                            last = nc.vector.scalar_tensor_tensor(dst[:, 1, f], d[:, f], col[:, c + f:c + f + 1],
                                                                  dst[:, 0, f].bitcast(F32), ALU.add, ALU.subtract)
                        last.then_inc(ev.sem(run), 1)
                elif kind == "th":
                    ev.wait(dve, run, step, part=1)
                    nc.vector.tensor_tensor(hT[:, s, 1], d, hT[:, s, 0].bitcast(F32), ALU.subtract
                                            ).then_inc(ev.sem(run), 1)
                elif kind == "v":
                    dense_full.wait(dve, run, step)
                    for t in range(TT):
                        last = nc.vector.tensor_tensor(
                            v_ones[:, s, t, :, 0:HD], d[:, t].rearrange("p (h e) -> p h e", h=H),
                            row[:, RI[f"bv{l}"]].rearrange("p (h e) -> p h e", h=H), ALU.add)
                    last.then_inc(ev.sem(run), 2)
                elif kind == "max":
                    hs, t, sp_, h = step[3:]
                    max_full.wait(dve, run, step)
                    if t == 0 and sp_ == 0 and h == 0:
                        neg_lo.wait_last(dve, run, step, lambda x: x[3] == hs)
                    c = 4 * h + 2 * sp_
                    nc.vector.tensor_reduce(m_tok[:, hs, t, c:c + 2], max_ps[:, max_full.number(run, step) % 2],
                                            AX.X, ALU.max).then_inc(max_taken.sem(run), 1)
                elif kind == "ng":
                    hs = step[3]
                    max_taken.wait(dve, run, step, ("max", l, s, hs, TT - 1, 1, HALVES - 1))
                    dense_full.wait_last(dve, run, step, lambda x: x[0] == "nm" and x[3] == hs)
                    for t in range(TT):
                        v4 = nm_tok[:, hs, t, 0:16].rearrange("p (h c k) -> p c h k", h=2, c=2)
                        m4 = m_tok[:, hs, t].rearrange("p (h k) -> p h k", h=2)
                        hi = v4[:, 0].bitcast(F32R)
                        if l == 1:
                            ins = nc.vector.tensor_scalar(hi, m4, -1.0, nan_col[:, t:t + 1], ALU.mult, ALU.add)
                        else:
                            ins = nc.vector.tensor_scalar(hi, m4, -1.0, None, ALU.mult)
                        ins.then_inc(neg_hi.sem(run), 1)
                    neg_hi.wait(dve, run, step)
                    for t in range(TT):
                        v4 = nm_tok[:, hs, t, 0:16].rearrange("p (h c k) -> p c h k", h=2, c=2)
                        m4 = m_tok[:, hs, t].rearrange("p (h k) -> p h k", h=2)
                        last = nc.vector.scalar_tensor_tensor(v4[:, 1], m4, -1.0, v4[:, 0], ALU.mult, ALU.subtract)
                    last.then_inc(neg_lo.sem(run), 1)
                elif kind == "pv":
                    n = pv_full.number(run, step) % 2
                    before = ("pv", l, s, step[3] - 1) if step[3] else None
                    pv_full.wait(dve, run, step)
                    hold()
                    turned_back.wait_ago(dve, run, step, 2)
                    nc.vector.transpose(pv_t[:, n], pv_ps[:, n, 0:S]).then_inc(pv_turned.sem(run), 1)
                    if before:
                        normalise(before)
                    pv_turned.wait(dve, run, step)
                    sums = pv_t[:, n].rearrange("p (b r) -> p b r", r=32)[:, :, HD:HD + 1]
                    nc.vector.reciprocal(inverse[:, n], sums).then_inc(inverted.sem(run), 1)
                    if before:
                        turn_back(before)
                elif kind == "oc":
                    normalise(("pv", l, s, GROUPS - 1))
                    turn_back(("pv", l, s, GROUPS - 1))
                elif kind == "o" or kind == "ff2":
                    dense_full.wait(dve, run, step)
                    res_ready.wait(dve, run, step, {("o", 0): ("rx", 0, s), ("ff2", 0): ("rs", 0, s),
                                                    ("o", 1): ("rs", 1, s), ("o", 2): ("rs", 3, s),
                                                    ("ff2", 1): ("rs", 4, s)}[kind, l])
                    if kind == "o":
                        stored[s].wait_last(dve, run, step)
                    nc.vector.tensor_tensor(y[:, s], d, res[:, s], ALU.add).then_inc(ev.sem(run), 2)
                elif kind == "ls":
                    src = {0: ("o", 0, s), 1: ("ff2", 0, s), 2: ("ln", 1, s), 3: ("o", 1, s), 4: ("o", 2, s)}[l]
                    if l == 2:
                        ln_done.wait(dve, run, step, src)
                    else:
                        evac(run, src).wait(dve, run, step, src)
                    for t in range(TT):
                        last = nc.vector.bn_stats(st[:, s, t], y[:, s, t])
                    last.then_inc(stats_part.sem(run), 1)
                    eps_added.wait_last(dve, run, step, lambda x: x[2] == s)
                    hold()
                    stats_part.wait(dve, run, step)
                    hold()
                    for t in range(TT):
                        last = nc.vector.bn_aggr(mv[:, s, t], st[:, s, t])
                    last.then_inc(stats.sem(run), 1)
                elif kind == "ln":
                    ln_done.wait_ago(dve, run, step)
                    hold()
                    stats.wait(dve, run, step, ("ls", l, s))
                    for t in range(TT):
                        last = nc.vector.scalar_tensor_tensor(z[:, t], y[:, s, t], mv[:, s, t, 0:1],
                                                              row[:, RI[f"g{l}"]], ALU.subtract, ALU.mult)
                    last.then_inc(scaled.sem(run), 1)
                    scaled.wait(dve, run, step)
                    rstd_ready.wait(dve, run, step, ("ls", l, s))
                    dst = y if l == 1 else hx
                    for t in range(TT):
                        last = nc.vector.scalar_tensor_tensor(dst[:, s, t], z[:, t], rstd[:, s, t:t + 1],
                                                              row[:, RI[f"be{l}"]], ALU.mult, ALU.add)
                    last.then_inc(ln_done.sem(run), 1)

        def tensor_steps(pe, run):
            def split_product(ps, w, mov, ahead_of_low=lambda: None):
                for n, (a, b) in enumerate([(0, 0), (1, 0), (0, 1)]):
                    if n == 2:
                        ahead_of_low()
                    for k in range(FT):
                        mm = nc.tensor.matmul(ps, w(a, k), mov(b, k), start=(n == 0 and k == 0),
                                              stop=(n == 2 and k == FT - 1))
                return mm

            for step in run.steps:
                kind, l, s = step[:3]

                def ready(key, part=0):
                    if not (is_dense(step) and bank(run, key) == bank(run, step)):
                        evac(run, key).wait(pe, run, step, key, part)

                if is_dense(step):
                    d = product(run, step)
                    evac(run, step).wait_ago(pe, run, step)
                if kind in ("tc", "tx", "th"):
                    if kind == "th":
                        ln_done.wait(pe, run, step, ("ln", {0: 0, 1: 2, 2: 3, 3: 4}[l], s))
                        src = hx[:, s]
                    else:
                        loaded[s].wait(pe, run, step, ("load", 0, s))
                        src = ctx_tok if kind == "tc" else x_tok
                    for f in range(FT):
                        for t in range(TT):
                            mm = nc.tensor.transpose(d[:, f, P * t:P * t + P], src[:, t, P * f:P * f + P], ident[:])
                    mm.then_inc(dense_full.sem(run), 1)
                elif kind == "q" and l == 0:
                    ready(("tx", 0, s))
                    for f in range(FT):
                        mm = nc.tensor.matmul(d[:, f], q0_w[:], xT[:, f], start=True, stop=True)
                    mm.then_inc(dense_full.sem(run), 1)
                elif kind in ("q", "k"):
                    w = 3 * (l - 1) + (kind == "k")
                    own = kind == "q" or l == 1
                    key = ("th", l, s) if own else ("tc", 0, s)
                    ready(key, part=1)
                    src = hT[:, s] if own else ctxT[:, s]
                    for f in range(FT):
                        mm = split_product(d[:, f], lambda a, k: qkv_w[:, w, a, k, P * f:P * f + P],
                                           lambda b, k: src[:, b, k], lambda: f == 0 and ready(key))
                    mm.then_inc(dense_full.sem(run), 1)
                elif kind == "v":
                    w = 3 * (l - 1) + 2
                    src = hT[:, s] if l == 1 else ctxT[:, s]
                    for t in range(TT):
                        mm = split_product(d[:, t], lambda a, k: src[:, a, k, P * t:P * t + P],
                                           lambda b, k: qkv_w[:, w, b, k])
                    mm.then_inc(dense_full.sem(run), 1)
                elif kind == "nm":
                    neg_lo.wait(pe, run, step, ("ng", l, s, step[3]))
                    dd = d.rearrange("p a q -> p (a q)")
                    for t in range(TT):
                        mm = nc.tensor.transpose(dd[:, P * t:P * t + P], nm_tok[:, step[3], t], ident[:])
                    mm.then_inc(dense_full.sem(run), 1)
                elif kind == "o":
                    compacted.wait(pe, run, step, ("oc", l, s))
                    for t in range(TT):
                        for k in range(FT):
                            mm = nc.tensor.matmul(d[:, t], attn[:, k, P * t:P * t + P], o_w[:, l, k],
                                                  start=(k == 0), stop=(k == FT - 1))
                    mm.then_inc(dense_full.sem(run), 1)
                elif kind == "ff1":
                    if step[3] == 0:
                        ready(("th", 3 * l, s), part=1)
                    for f in range(2):
                        m = 2 * step[3] + f
                        mm = split_product(d[:, f], lambda a, k: ff1_w[:, l, a, k, P * m:P * m + P],
                                           lambda b, k: hT[:, s, b, k],
                                           lambda: m == 0 and ready(("th", 3 * l, s)))
                    mm.then_inc(dense_full.sem(run), 1)
                elif kind == "ff2":
                    last_two = [("ff1", l, s, c) for c in range(NF // 2 - 2, NF // 2)]
                    if bank(run, last_two[0]) != bank(run, last_two[1]):
                        ready(last_two[0])
                    ready(last_two[1])
                    for t in range(TT):
                        for k in range(NF):
                            mm = nc.tensor.matmul(d[:, t], hid[:, k, P * t:P * t + P], ff2_w[:, l, k],
                                                  start=(k == 0), stop=(k == NF - 1))
                    mm.then_inc(dense_full.sem(run), 1)
                elif kind == "max":
                    hs, t, sp_, h = step[3:]
                    if hs == 0 and t == 0 and sp_ == 0 and h == 0:
                        q_stacked[s].wait(pe, run, step, ("stq", l, s))
                        k_stacked[s].wait(pe, run, step, ("stk", l, s))
                        if l < 2:
                            mask_row[s].wait(pe, run, step, ("r0", l, s))
                    n = max_full.number(run, step) % 2
                    max_taken.wait_ago(pe, run, step, 2)
                    if l == 1:
                        nc.tensor.matmul(max_ps[:, n], ident_bf[:], bias_qk[:, t:t + 1].to_broadcast([P, 2, S]),
                                         start=True, stop=False)
                    for k in range(2):
                        slot = 4 * hs + 2 * sp_ + k
                        rows_ = slice(HROWS * h, HROWS * h + K_MAXPASS)
                        mm = nc.tensor.matmul(max_ps[:, n, k], q_stack[rows_, s, slot, P * t:P * t + P],
                                              k_stack[rows_, s, slot], start=(l != 1),
                                              stop=(l != 1 or k == 1))
                    mm.then_inc(max_full.sem(run), 1)
                elif kind == "exp":
                    g, kt, h = step[3:]
                    if g % 2 == 0 and kt == 0 and h == 0:
                        max_rows[g // 2].wait(pe, run, step, ("nm", l, s, g // 2))
                    n = exp_full.number(run, step) % 2
                    probs_ready.wait_ago(pe, run, step, 2)
                    if l == 1:
                        nc.tensor.matmul(exp_ps[:, n], ident_bf[:], bias_kq[:, kt:kt + 1].to_broadcast([P, 2, S]),
                                         start=True, stop=False)
                    for k in range(2):
                        slot = 2 * g + k
                        rows_ = slice(HROWS * h, HROWS * h + K_EXPPASS)
                        mm = nc.tensor.matmul(exp_ps[:, n, k], k_stack[rows_, s, slot, P * kt:P * kt + P],
                                              q_stack[rows_, s, slot], start=(l != 1),
                                              stop=(l != 1 or k == 1))
                    mm.then_inc(exp_full.sem(run), 1)
                elif kind == "pv":
                    g = step[3]
                    probs_ready.wait(pe, run, step, ("exp", l, s, g, TT - 1, HALVES - 1))
                    if g == 0:
                        if l == 0:
                            pool_v.wait(pe, run, step, ("v0", 0, s))
                        else:
                            ready(("v", l, s))
                    n = pv_full.number(run, step) % 2
                    pv_turned.wait_ago(pe, run, step, 2)
                    for kt in range(TT):
                        for j in range(4):
                            h, k = j // 2, j % 2
                            head = SLOTS * h + 2 * g + k
                            mm = nc.tensor.matmul(pv_ps[32 * j:32 * j + 32, n, 0:S],
                                                  v_ones[:, s, kt, head, :], probs[:, g % 2, 4 * h + 2 * kt + k],
                                                  start=(kt == 0), stop=(kt == TT - 1))
                    mm.then_inc(pv_full.sem(run), 1)


        opening = Run(OPENING)
        closing = Run(CLOSING)

        with nc.Block() as block:
            @block.sync
            def _(sp):
                sp.dma_start(ident[:], ident_in).then_inc(s_const, 16)
                sp.dma_start(row[:].rearrange("p r e -> p (r e)"),
                             rows.partition_broadcast(P)).then_inc(s_const, 16)
                sp.dma_start(col[:], cols).then_inc(s_const, 16)
                sp.dma_start(y[:, 0, 0, 0:P], same_slot).then_inc(s_const, 16)
                sp.dma_start(y[:, 0, 0, P:2 * P], same_head).then_inc(s_const, 16)
                sp.dma_start(y[:, 0, 1, 0:P], wv_rep).then_inc(s_const, 16)
                sp.dma_start(z[0:HD, 0, 0:P], wq_rep).then_inc(s_const, 16)
                sp.dma_start(z[0:HD, 0, P:2 * P], wk_rep).then_inc(s_const, 16)
                sp.dma_start(hx[0:B, 0, 0, :].bitcast(I32), mask0).then_inc(s_const, 16)
                sp.dma_start(x_tok[:, :, 0:S // 4].bitcast(I32), mask1.rearrange("(t p) k -> p t k", p=P)
                             ).then_inc(s_const, 16)
                sp.dma_start(attn[:], w_out.rearrange("(t p) e -> p t e", p=P)).then_inc(s_const, 16)
                for n, (_, _, src, k, _, stage) in enumerate(splits):
                    sp.dma_start(stage.rearrange("p (t e) -> p t e", t=k), src.rearrange("(t p) e -> p t e", p=P)
                                 ).then_inc(s_raw[n], 16)
                for l in range(2):
                    sp.dma_start(o_w[:, l + 1], wo[l].rearrange("(t p) e -> p t e", p=P)).then_inc(s_plain, 16)
                    sp.dma_start(ff2_w[:, l], wff2[l].rearrange("(t p) e -> p t e", p=P)).then_inc(s_plain, 16)
                sp.wait_ge(s_dve, 6)
                sp.dma_start(masks_dram[0:B], hx[0:B, 0, 1, :]).then_inc(s_const, 16)
                sp.dma_start(masks_dram[B:B + 1], z[0:1, 1, :]).then_inc(s_const, 16)
                ones = v_ones[:].rearrange("p s t h e -> p (s t h e)").rearrange("p (k q) -> p k q", k=SLOTS)
                for s in range(LANES):
                    for h in range(HALVES):
                        sp.dma_start(q_stack[HROWS * h:HROWS * h + 1, s].bitcast(F32), ones[0:1]).then_inc(s_const, 16)
                        sp.dma_start(k_stack[HROWS * h + R_MAX:HROWS * h + R_MAX + 2, s].bitcast(F32),
                                     ones[0:2]).then_inc(s_const, 16)
                sp.wait_ge(s_const, 16 * SETUP_DMAS)
                sp.wait_ge(s_plain, 16 * SETUP_PLAIN)
                sp.wait_ge(primed, 1)
                sp.wait_ge(s_act, SETUP_ACT)
                sp.wait_ge(s_dve, SETUP_DVE)

                sync_steps(sp, opening)
                finish_dmas(sp, opening)

            @block.gpsimd
            def _(pool):
                for sg in every:
                    pool.sem_inc(sg.sems[1], sg.per)
                pool.sem_inc(primed, 1)
                pool.wait_ge(s_act, SETUP_ACT)
                pool.wait_ge(s_dve, SETUP_DVE)
                pool.wait_ge(s_const, 16 * SETUP_DMAS)

                pool_steps(pool, opening)

            @block.scalar
            def _(act):
                for n, (hi, _, _, _, scale, stage) in enumerate(splits):
                    act.wait_ge(s_raw[n], 16)
                    nc.scalar.activation(hi, stage, ACT.Copy, scale=scale).then_inc(s_hi, 1)
                act.wait_ge(s_pe, 1)
                nc.scalar.activation(o_w[:, 0], dense_ps[:, 1], ACT.Copy).then_inc(s_act, 1)
                act.wait_ge(s_pe, 2)
                nc.scalar.activation(bias_kq[:], max_ps[:, 0], ACT.Copy).then_inc(s_act, 1)
                act.wait_ge(primed, 1)
                act.wait_ge(s_dve, SETUP_DVE)

                scalar_steps(act, opening)

            @block.vector
            def _(dve):
                waits = [0]

                def chain(ins):
                    waits[0] += 1
                    ins.then_inc(s_dve, 1)
                    dve.wait_ge(s_dve, waits[0])
                chain(nc.vector.memset(v_ones[:], 1.0))
                chain(nc.vector.memset(nm_tok[:], 0.0))
                chain(nc.vector.memset(minus_half[:], -0.5))
                chain(nc.vector.memset(z[0:1, 1, :], 0.0))
                dve.wait_ge(s_const, 16 * SETUP_LOADS)
                chain(nc.vector.tensor_copy(hx[0:B, 0, 1, :], hx[0:B, 0, 0, :].bitcast(I32)))
                chain(nc.vector.tensor_scalar(hx[0:B, 0, 1, :].bitcast(F32R), hx[0:B, 0, 1, :], 0.0, L0_MASKED,
                                              ALU.is_equal, ALU.mult))
                chain(nc.vector.tensor_copy(ctx_tok[:], x_tok[:].bitcast(U8)[:, :, 0:S]))
                chain(nc.vector.tensor_scalar(ctx_tok[:], ctx_tok[:], 0.0, L1_MASKED, ALU.is_equal, ALU.mult))
                chain(nc.vector.tensor_copy(bias_qk[:], ctx_tok[:]))
                chain(nc.vector.tensor_copy(ident_bf[:], ident[:]))
                chain(nc.vector.tensor_reduce(nan_col[:], ctx_tok[:], AX.X, ALU.max))
                chain(nc.vector.tensor_scalar(nan_col[:], nan_col[:], 1e30, None, ALU.mult))
                chain(nc.vector.tensor_tensor(nan_col[:], nan_col[:], nan_col[:], ALU.subtract))
                chain(nc.vector.tensor_scalar(col[:, C_Q:C_Q + 4], col[:, C_Q:C_Q + 4], 0.25, None, ALU.mult))
                chain(nc.vector.tensor_tensor(y[:, 0, 1, 0:P], y[:, 0, 1, 0:P], y[:, 0, 0, P:2 * P], ALU.mult))
                dve.wait_ge(s_pe, 1)
                chain(nc.vector.scalar_tensor_tensor(q0_w[:], dense_ps[:, 0, 0, 0:P], 1.0 / 16.0, y[:, 0, 0, 0:P],
                                                     ALU.mult, ALU.mult))
                assert waits[0] == SETUP_DVE_CHAIN, waits[0]
                for n, (hi, lo, _, _, scale, stage) in enumerate(splits):
                    dve.wait_ge(s_hi, n + 1)
                    nc.vector.scalar_tensor_tensor(lo, stage, scale, hi.bitcast(F32), ALU.mult, ALU.subtract
                                                   ).then_inc(s_lo, 1)
                dve.wait_ge(s_lo, len(splits))
                dve.sem_inc(s_dve, 1)
                dve.wait_ge(s_act, SETUP_ACT)
                dve.wait_ge(primed, 1)
                dve.wait_ge(s_const, 16 * SETUP_DMAS)

                vector_steps(dve, opening)

            @block.tensor
            def _(pe):
                pe.wait_ge(s_const, 16 * SETUP_LOADS)
                pe.wait_ge(s_dve, SETUP_DVE_CHAIN - 1)
                nc.tensor.matmul(dense_ps[:, 0, 0, 0:P], z[0:HD, 0, 0:P], z[0:HD, 0, P:2 * P], start=True, stop=True)
                for t in range(FT):
                    last = nc.tensor.matmul(dense_ps[:, 1, t], y[:, 0, 1, 0:P], attn[:, t], start=True, stop=True)
                last.then_inc(s_pe, 1)
                for kt in range(TT):
                    for t in range(TT):
                        last = nc.tensor.transpose(max_ps[:, 0, kt, P * t:P * t + P], ctx_tok[:, t, P * kt:P * kt + P],
                                                   ident[:])
                last.then_inc(s_pe, 1)
                pe.wait_ge(s_act, SETUP_ACT)
                pe.wait_ge(s_dve, SETUP_DVE)
                pe.wait_ge(s_const, 16 * SETUP_DMAS)
                pe.wait_ge(s_plain, 16 * SETUP_PLAIN)
                pe.wait_ge(primed, 1)

                tensor_steps(pe, opening)

        with nc.Block() as block:
            @block.sync
            def _(sp):
                with sp.Fori(0, N_LOOP) as i:
                    sync_steps(sp, Run(LOOP, i))
                finish_dmas(sp, Run(LOOP, 0))

            @block.gpsimd
            def _(pool):
                with pool.Fori(0, N_LOOP) as i:
                    pool_steps(pool, Run(LOOP, i))

            @block.scalar
            def _(act):
                with act.Fori(0, N_LOOP) as i:
                    scalar_steps(act, Run(LOOP, i))

            @block.vector
            def _(dve):
                with dve.Fori(0, N_LOOP) as i:
                    vector_steps(dve, Run(LOOP, i))

            @block.tensor
            def _(pe):
                with pe.Fori(0, N_LOOP) as i:
                    tensor_steps(pe, Run(LOOP, i))

        with nc.Block() as block:
            @block.sync
            def _(sp):
                sync_steps(sp, closing)
                finish_dmas(sp, closing)

            @block.gpsimd
            def _(pool):
                pool_steps(pool, closing)

            @block.scalar
            def _(act):
                scalar_steps(act, closing)

            @block.vector
            def _(dve):
                vector_steps(dve, closing)

            @block.tensor
            def _(pe):
                tensor_steps(pe, closing)


def kernel(**inputs):
    import numpy as _np
    import concourse.bacc as _bacc
    from concourse import mybir as _mybir
    from concourse.bass_utils import run_bass_kernel_spmd as _run

    a = {k: _np.asarray(v) for k, v in inputs.items()}
    f, s, d, g, j = 2, 8, 16, 4, 2
    nat = _np.arange(256)
    ds = nat.reshape(f, s, d).transpose(0, 2, 1).reshape(-1)
    comp = nat.reshape(f, g, j, d).transpose(0, 2, 3, 1).reshape(-1)
    L0, L1 = "L0_xattn_", "L1_xattn_"

    def tiles(v):
        return v.reshape(-1, 128).T

    ins = {
        "x": a["x"],
        "ctx_in": a["ctx_1024"][:, :, ds],
        "mask0": a["mask_Bx1x1xS2_if1"].reshape(16, 256),
        "mask1": a["mask_1x1xSxS_bk0"].reshape(256, 256).view(_np.int32),
        "wq_rep": _np.tile(a[L0 + "wq"].T, (1, s)),
        "wk_rep": _np.repeat(a[L0 + "wk"].T, s, axis=1),
        "wv_rep": _np.tile(_np.repeat(_np.repeat(a[L0 + "wv"].T, g, 0), g, 1), (j, j)),
        "w_out": a[L0 + "w_out"][comp],
        "wq1": a[L1 + "sa_wq"][:, ds], "wk1": a[L1 + "sa_wk"][:, ds], "wv1": a[L1 + "sa_wv"],
        "wq2": a[L1 + "ca_wq"][:, ds], "wk2": a[L1 + "ca_wk"][ds][:, ds], "wv2": a[L1 + "ca_wv"][ds],
        "wo1": a[L1 + "sa_wo"][comp], "wo2": a[L1 + "ca_wo"][comp],
        "wf1_0": a[L0 + "w_ff1"], "wf1_1": a[L1 + "ff_w1"],
        "wf2_0": a[L0 + "w_ff2"], "wf2_1": a[L1 + "ff_w2"],
        "rows": _np.stack([a[L0 + "g1"], a[L0 + "beta1"], a[L0 + "g2"], a[L0 + "beta2"],
                           a[L1 + "ln1_g"], a[L1 + "ln1_b"], a[L1 + "ln2_g"], a[L1 + "ln2_b"],
                           a[L1 + "ln3_g"], a[L1 + "ln3_b"],
                           a[L0 + "b_out"], a[L0 + "b_ff2"], a[L1 + "sa_bo"], a[L1 + "ca_bo"], a[L1 + "ff_b2"],
                           a[L1 + "sa_bv"], a[L1 + "ca_bv"]]).reshape(-1),
        "cols": _np.concatenate([tiles(a[L1 + "sa_bq"][ds]), tiles(a[L1 + "ca_bq"][ds]), tiles(a[L1 + "sa_bk"][ds]),
                                 tiles(a[L1 + "ca_bk"][ds]), tiles(a[L0 + "b_ff1"]), tiles(a[L1 + "ff_b1"])], 1),
    }
    slot_k, slot_m = nat[:128] // d, nat[:128] % s
    head = (nat[:128] // 64) * g + nat[:128] % g
    ins["ident"] = _np.eye(128, dtype=_np.float32)
    ins["same_slot"] = (slot_k[:, None] == slot_m[None, :]).astype(_np.float32)
    ins["same_head"] = (head[:, None] == head[None, :]).astype(_np.float32)

    nc = _bacc.Bacc("TRN2", target_bir_lowering=False, num_devices=1, dynamic_dma_scratch_size=1024)
    arrays, ap = {}, {}
    for name, v in ins.items():
        arrays[f"in_{name}"] = _np.ascontiguousarray(v)
        ap[name] = nc.dram_tensor(f"in_{name}", v.shape, _mybir.dt.from_np(v.dtype), kind="ExternalInput").ap()
    out = nc.dram_tensor("out_0", (16, 256, 256), _mybir.dt.float32, kind="ExternalOutput").ap()
    masks = nc.dram_tensor("masks_dram", (17, 256), _mybir.dt.float32, kind="Internal").ap()
    build(nc, ap["x"], ap["ctx_in"], ap["mask0"], ap["mask1"], ap["wq_rep"], ap["wk_rep"], ap["wv_rep"], ap["w_out"],
          [ap[n] for n in ("wq1", "wk1", "wv1", "wq2", "wk2", "wv2")], [ap["wo1"], ap["wo2"]],
          [ap["wf1_0"], ap["wf1_1"]], [ap["wf2_0"], ap["wf2_1"]], ap["rows"], ap["cols"], ap["ident"],
          ap["same_slot"], ap["same_head"], out, masks)
    r = _run(nc, [arrays], core_ids=[0])
    return r.results[0]["out_0"]
```
